# Optimizing a Trainium2 kernel written in Bass

```python
import numpy as np
import jax
import jax.numpy as jnp

def _softmax(x, axis=-1):
    return jax.nn.softmax(x, axis=axis)

def _gelu(x):
    return jax.nn.gelu(x, approximate=True)

def _silu(x):
    return jax.nn.silu(x)

def _sigmoid(x):
    return jax.nn.sigmoid(x)

def _layernorm(x, axis=-1, eps=1e-05):
    m = jnp.mean(x, axis=axis, keepdims=True)
    v = jnp.var(x, axis=axis, keepdims=True)
    return (x - m) / jnp.sqrt(v + eps)

def _scatter_add(tgt, idx, src, axis=0):
    return tgt.at[idx].add(src)

def _segment_sum(src, seg, n):
    return jax.ops.segment_sum(src, seg, n)
kernel_name = 'mk_prb_d1_jaxref_r8_0e9f28'

def setup_inputs(seed: int=0):
    np.random.seed(seed)
    _w = jnp.asarray

    def _L0_attn_setup():
        import jax, jax.numpy as jnp
        import numpy as np
        N_EMBD = 128
        N_HEAD = 16
        HEAD_DIM = N_EMBD // N_HEAD
        LATENT_DIM = N_EMBD // 2
        B, T = (4, 256)
        key = jax.random.key(seed)
        ks = jax.random.split(key, 5)

        def init(k, fan_in, fan_out):
            bound = 1.0 / np.sqrt(fan_in)
            return jax.random.uniform(k, (fan_in, fan_out), jnp.float32, -bound, bound)
        return {'x': jax.random.normal(ks[0], (B, T, N_EMBD), jnp.float32), 'Wc_down': init(ks[1], N_EMBD, LATENT_DIM), 'Wq_up': init(ks[2], LATENT_DIM, N_EMBD), 'Wkv_up': init(ks[3], LATENT_DIM, 2 * HEAD_DIM), 'Wc_proj': init(ks[4], N_EMBD, N_EMBD)}
    _L0_attn_in = _L0_attn_setup()

    def _L0_ffn_setup():
        import jax, jax.numpy as jnp
        import numpy as np
        B, S, D = (2, 256, 128)
        E, K, DFF = (8, 2, 4 * 128)
        EPS_GATE = 1e-08
        EPS_LN = 1e-05
        key = jax.random.key(seed)
        ks = jax.random.split(key, 4)
        scaled = lambda k, shape, fan: jax.random.normal(k, shape, jnp.float32) / np.sqrt(fan).astype(np.float32)
        return {'x': jax.random.normal(ks[0], (B, S, D), jnp.float32), 'Wg': scaled(ks[1], (D, E), D), 'bg': jnp.zeros((E,), jnp.float32), 'W1': scaled(ks[2], (E, D, DFF), D), 'b1': jnp.zeros((E, DFF), jnp.float32), 'W2': scaled(ks[3], (E, DFF, D), DFF), 'b2': jnp.zeros((E, D), jnp.float32), 'gamma': jnp.ones((D,), jnp.float32), 'beta': jnp.zeros((D,), jnp.float32)}
    _L0_ffn_in = _L0_ffn_setup()
    _d = {'L0_attn_x': _L0_attn_in['x'], 'L0_attn_Wc_down': _L0_attn_in['Wc_down'], 'L0_attn_Wq_up': _L0_attn_in['Wq_up'], 'L0_attn_Wkv_up': _L0_attn_in['Wkv_up'], 'L0_attn_Wc_proj': _L0_attn_in['Wc_proj'], 'L0_ffn_Wg': _L0_ffn_in['Wg'], 'L0_ffn_bg': _L0_ffn_in['bg'], 'L0_ffn_W1': _L0_ffn_in['W1'], 'L0_ffn_b1': _L0_ffn_in['b1'], 'L0_ffn_W2': _L0_ffn_in['W2'], 'L0_ffn_b2': _L0_ffn_in['b2'], 'L0_ffn_gamma': _L0_ffn_in['gamma'], 'L0_ffn_beta': _L0_ffn_in['beta']}
    _x0 = _d['L0_attn_x']
    _d['L0_attn_x'] = jax.random.normal(jax.random.fold_in(jax.random.key(seed), 1), (16, 512, 128), dtype=_x0.dtype)
    del _x0
    return _d

def reference(L0_attn_x, L0_attn_Wc_down, L0_attn_Wq_up, L0_attn_Wkv_up, L0_attn_Wc_proj, L0_ffn_Wg, L0_ffn_bg, L0_ffn_W1, L0_ffn_b1, L0_ffn_W2, L0_ffn_b2, L0_ffn_gamma, L0_ffn_beta):

    def _L0_attn_ref(x, Wc_down, Wq_up, Wkv_up, Wc_proj):
        import jax, jax.numpy as jnp
        import numpy as np
        N_EMBD = 128
        N_HEAD = 16
        HEAD_DIM = N_EMBD // N_HEAD
        LATENT_DIM = N_EMBD // 2
        B, T = (4, 256)
        Bsz, Tlen, C = x.shape
        latent = x @ Wc_down
        q = (latent @ Wq_up).reshape(Bsz, Tlen, N_HEAD, HEAD_DIM)
        kv = latent @ Wkv_up
        k, v = (kv[..., :HEAD_DIM], kv[..., HEAD_DIM:])
        scale = 1.0 / np.sqrt(HEAD_DIM)
        att = jnp.einsum('bthd,bsd->bhts', q, k) * scale
        causal = jnp.tril(jnp.ones((Tlen, Tlen), dtype=bool))
        att = jnp.where(causal[None, None], att, -jnp.inf)
        att = jax.nn.softmax(att, axis=-1)
        y = jnp.einsum('bhts,bsd->bthd', att, v).reshape(Bsz, Tlen, C)
        return y @ Wc_proj

    def _L0_ffn_ref(x, Wg, bg, W1, b1, W2, b2, gamma, beta):
        import jax, jax.numpy as jnp
        import numpy as np
        B, S, D = (2, 256, 128)
        E, K, DFF = (8, 2, 4 * 128)
        EPS_GATE = 1e-08
        EPS_LN = 1e-05
        b, s, d = x.shape
        xf = x.reshape(-1, d)
        T = xf.shape[0]
        num_experts = Wg.shape[1]
        logits = xf @ Wg + bg
        w = jax.nn.softmax(logits, axis=-1)
        top_w, top_idx = jax.lax.top_k(w, K)
        top_w = top_w / (top_w.sum(axis=-1, keepdims=True) + EPS_GATE)
        cw = jnp.zeros((T, num_experts), xf.dtype).at[jnp.arange(T)[:, None], top_idx].add(top_w)
        out = jnp.zeros_like(xf)
        for e in range(num_experts):
            h = jax.nn.gelu(xf @ W1[e] + b1[e], approximate=False)
            y = h @ W2[e] + b2[e]
            out = out + cw[:, e:e + 1] * y
        mu = out.mean(axis=-1, keepdims=True)
        var = out.var(axis=-1, keepdims=True)
        out = (out - mu) / jnp.sqrt(var + EPS_LN) * gamma + beta
        return out.reshape(b, s, d)
    x = L0_attn_x
    xn = _layernorm(x, axis=-1)
    x = x + _L0_attn_ref(xn, L0_attn_Wc_down, L0_attn_Wq_up, L0_attn_Wkv_up, L0_attn_Wc_proj) + _L0_ffn_ref(xn, L0_ffn_Wg, L0_ffn_bg, L0_ffn_W1, L0_ffn_b1, L0_ffn_W2, L0_ffn_b2, L0_ffn_gamma, L0_ffn_beta)
    return x

_drawn_inputs = setup_inputs


def setup_inputs(seed=0):
    import zlib

    import numpy as np

    out = dict(_drawn_inputs(seed))
    spreads = {'L0_ffn_bg': (0.0, 0.435),
     'L0_ffn_b1': (0.0, 0.8),
     'L0_ffn_b2': (0.0, 0.605),
     'L0_ffn_gamma': (1.0, 0.6),
     'L0_ffn_beta': (0.0, 0.8)}
    factors = {'L0_attn_Wc_down': 3.915,
     'L0_attn_Wq_up': 8.0,
     'L0_attn_Wkv_up': 3.992,
     'L0_attn_Wc_proj': 3.981}
    for name, (base, spread) in spreads.items():
        noise = np.random.default_rng([zlib.crc32(name.encode()), seed]).standard_normal(out[name].shape)
        drawn = base * np.exp(spread * noise) if base else spread * noise
        out[name] = jnp.asarray(drawn.astype(out[name].dtype))
    for name, factor in factors.items():
        out[name] = (out[name] * factor).astype(out[name].dtype)
    return out
```

```python
from contextlib import ExitStack

import concourse.bass as bass
from concourse import mybir

F32 = mybir.dt.float32
F32R = mybir.dt.float32r
BF16 = mybir.dt.bfloat16
ALU = mybir.AluOpType
ACT = mybir.ActivationFunctionType
AX_X = mybir.AxisListType.X

P = 128
D = 128
NB = 16
T = 512
TT = T // P
NT = NB * TT
H = 16
DH = D // H
LAT = 64
G = 4
NJ = H // G
NSTEP = NB * NJ
E = 8
F = 512
FC = F // P
NC = E * FC
SCALE = 1.0 / float(DH) ** 0.5
EPS_LN = 1e-5
EPS_GATE = 1e-8

C_ID = 0
C_CAUSAL = C_ID + P
C_CAUSALT = C_CAUSAL + P
C_NEGQ = C_CAUSALT + P
C_NEGK = C_NEGQ + 1
C_ONEK = C_NEGK + 1
C_HALF = C_ONEK + 1
C_LESS = C_HALF + TT
C_END = C_LESS + E * E

R_MAX = 3 * DH
EX_UNITS = ((0, 0), (0, 2), (1, 0), (1, 2), (2, 0), (3, 0))
EX_HEADS = (2, 2, 2, 2, 4, 4)
LW2 = 2
MX_UNITS = ((0, 0, 4), (1, 0, 2), (1, 2, 2)) + tuple((i, g, 1) for i in (2, 3) for g in range(G))
NMX = len(MX_UNITS)
NEX = len(EX_UNITS)


def build(nc, x, wcd, wqu, wkvu, wcp, wg, bg, w1, b1, w2, b2, gamma, beta, const, selc, resid, out):
    with ExitStack() as ctx:
        def sb(name, shape, dt=F32, scope=ctx):
            return scope.enter_context(nc.sbuf_tensor(name, shape, dt))

        def sem(name):
            return ctx.enter_context(nc.semaphore(name))

        cst = sb("cst", [P, C_END])
        causal_b = sb("causal_b", [P, 4 * P], BF16)
        causal_t = sb("causal_t", [P, 4 * P], BF16)
        ident_b = sb("ident_b", [P, P], BF16)
        xin = sb("xin", [P, 2, T])
        xT = sb("xT", [P, NT * P])
        w1h = sb("w1h", [P, NC * P], F32R)
        w1l = sb("w1l", [P, NC * P], F32R)
        w2h = sb("w2h", [P, NC * P], F32R)
        w2l = sb("w2l", [P, NC * P], F32R)
        gam = sb("gam", [P, D])
        bet = sb("bet", [P, D])
        b1r = sb("b1r", [NC, P])
        b1T = sb("b1T", [P, NC])
        b2r = sb("b2r", [2 * E, D])
        b2h = sb("b2h", [2 * E, D], F32R)
        b2l = sb("b2l", [2 * E, D], F32R)
        bgc = sb("bgc", [E, 1])
        cwhl = sb("cwhl", [P, NT, 2 * E])
        ident = cst[:, C_ID:C_ID + P]

        scope_a = ExitStack()
        A = lambda name, shape, dt=F32: sb(name, shape, dt, scope_a)
        wcd_s = A("wcd_s", [P, LAT])
        wcdT = A("wcdT", [LAT, P])
        wup = A("wup", [LAT, D + 2 * DH])
        wcp_s = A("wcp_s", [P, D])
        wg_s = A("wg_s", [P, E])
        wgh = A("wgh", [P, E], F32R)
        wgl = A("wgl", [P, E], F32R)
        wfold = A("wfold", [P, D + 2 * DH])
        wst = A("wst", [P, NJ + 1, P])
        wsth = A("wsth", [P, NJ + 1, P], F32R)
        wstl = A("wstl", [P, NJ + 1, P], F32R)
        stats = A("stats", [P, 2, TT, 6])
        mv = A("mv", [P, 2, TT, 2])
        veps = A("veps", [P, 2, TT])
        rstd = A("rstd", [P, 2, TT])
        xn = A("xn", [P, 2, T])
        xh = A("xh", [P, 2, T], F32R)
        xl = A("xl", [P, 2, T], F32R)
        lgT = A("lgT", [E, 2, T])
        w_r = A("w_r", [P, NT, E])
        w_c = A("w_c", [P, NT, E])
        rsm = A("rsm", [P, NT])
        rsr = A("rsr", [P, NT])
        rank = A("rank", [P, NT, E])
        kpad = A("kpad", [P, 2, G, T], F32R)
        kh = A("kh", [P, T], F32R)
        kvs = A("kvs", [P, T])
        vv = A("vv", [P, 2, TT, 32])
        qs = A("qs", [P, 4, T], F32R)
        qh = A("qh", [P, 2, T], F32R)
        pp = A("pp", [P, 2, G, T])
        pvs = A("pvs", [P, T])
        rden = A("rden", [P, TT * G])
        y = A("y", [P, 2, TT, D])
        yT = A("yT", [P, T])
        nm = A("nm", [P, TT, G])
        nmhl = A("nmhl", [P, 2, TT, 2, G])
        nmh_r = A("nmh_r", [P, TT, G], F32R)
        ms = A("ms", [2 * G, 2, T], F32R)
        cwh_r = A("cwh_r", [P, NT, E], F32R)
        cmpa = pp[:, 0, :, :].rearrange("p g t -> p (g t)")
        cmpb = pp[:, 1, :, :].rearrange("p g t -> p (g t)")
        scope_a.close()

        scope_b = ExitStack()
        B = lambda name, shape, dt=F32: sb(name, shape, dt, scope_b)
        zh = B("zh", [P, 2, T], F32R)
        zl = B("zl", [P, 2, T], F32R)
        selcw = B("selcw", [P, E * P])
        selr = B("selr", [P, E * P], F32R)
        cws = B("cws", [P, T], F32R)
        cwb = B("cwb", [P, 2, T])
        hf = B("hf", [P, 4, T])
        hh = B("hh", [P, 4, T], F32R)
        hl = B("hl", [P, 4, T], F32R)
        yw = B("yw", [P, 2, T])
        facc = B("facc", [P, T])
        fst = B("fst", [P, TT, 6])
        fmv = B("fmv", [P, TT, 2])
        fve = B("fve", [P, TT])
        frs = B("frs", [P, TT])
        fz = B("fz", [P, T])
        cwst = B("cwst", [P, TT * 2 * E])
        fo = B("fo", [P, 2, T])
        scope_b.close()

        ps = ctx.enter_context(nc.psum_tensor("ps", [P, 8, T], F32))
        PS_MX, PS_EX, PS_PV, PS_MISC = 0, 2, 6, 7
        misc = ps[:, PS_MISC, :]

        dma_names = ("cst", "wcd", "wqu", "wkvu", "wcp", "wg", "bg", "w1", "b1", "w2", "b2", "gam", "bet", "sel")
        ld = {n: sem(f"s_ld_{n}") for n in dma_names}
        s_x = [sem(f"s_x{i}") for i in range(2)]
        s_xa = [sem(f"s_xa{i}") for i in range(2)]
        s_xr = [sem(f"s_xr{i}") for i in range(2)]
        s_xb = [sem(f"s_xb{i}") for i in range(2)]
        names = ("const_b", "wcdT_ps", "wcdT", "fold_ps", "fold", "wst0", "wst", "wsth", "wstl", "wgh", "wgl", "kz",
                 "kone", "vz", "vone", "w1h", "w1l", "w2h", "w2l", "b1_ps", "b1T", "b2h", "b2l",
                 "stat", "mv", "veps", "rstd", "xn", "xT_ps", "xT", "xh0", "xl0", "lg_ps", "lgT", "lt_ps", "lt",
                 "rt", "rexp", "cw",
                 "xh", "xl", "kv_ps", "kh", "kvs", "kpad", "v_ps", "v", "q_ps", "qh", "qs", "mx_ps", "mx", "nm1",
                 "nm", "mT_ps", "mT", "ex_ps", "ex", "pv", "pvs", "pvT_ps", "rden", "y", "yT_ps", "yT",
                 "c_ps", "xo",
                 "cz", "selr", "zh", "zl", "cwst", "ct_ps", "cws", "cb_ps", "cwb", "h_ps", "hf", "hh_a", "hh_d", "hl",
                 "y_ps", "yw", "fadd", "ft_ps", "fst", "fmv", "fve", "frs", "fz", "fg", "fb", "fo", "zero")
        s = {n: sem(f"s_{n}") for n in names}
        s_passed = sem("s_passed")
        s_mrow = [sem(f"s_mrow{i}") for i in range(4)]
        s_out = [sem(f"s_out{i}") for i in range(2)]

        x_v = x.rearrange("b (i p) d -> b p i d", p=P)
        out_v = out.rearrange("b (i p) d -> b p i d", p=P)
        resid_v = resid.rearrange("b (i p) d -> b p i d", p=P)

        def seq_rows(view, b):
            return view[b, :, :, :] if isinstance(b, int) else \
                view[bass.ds(b, 1), :, :, :].rearrange("a p i d -> p (a i) d")

        def stage(it, u, lag, n_all, unroll, per=1):
            assert (u - lag) % per == 0
            n = it * (unroll // per) + (u - lag) // per
            if isinstance(it, int) and not 0 <= n < n_all:
                return None
            return n

        def trips(eng, body, head=1):
            for it in range(head):
                body(it)
            with eng.Fori(head, NB // 2 - 1) as it:
                body(it)
            body(NB // 2 - 1)

        def loops(eng, body, lags, n_steps, unroll, head=1):
            total = -(-(n_steps + max(lags)) // unroll)
            full = n_steps // unroll
            for it in range(head):
                body(it)
            with eng.Fori(head, full) as it:
                body(it)
            for it in range(full, total):
                body(it)

        block = ctx.enter_context(nc.Block())

        LAG0 = dict(x=0, xT=1, lg=2, lt=3)
        LAGA = dict(kv=0, v=1, q=1, mx=2, m=3, ex=4, pvT=5, yT=10, c=11)
        XSLOT = {0: ("kv", 0), 1: ("v", 1), 2: ("yT", 10), 3: ("c", 11)}

        def a_idx(it, u, what):
            per = 4 if what in ("kv", "v", "yT", "c") else 1
            return stage(it, u, LAGA[what], NB if per == 4 else NSTEP, 8, per)

        def a_par(u, what):
            per = 4 if what in ("kv", "v", "yT", "c") else 1
            return (u - LAGA[what]) // per

        def plain(eng):
            eng.sem_inc(s_passed, 1)

        def pair(b, it, u, what):
            return b // 2 if isinstance(b, int) else it + a_par(u, what) // 2

        def misc_freed(it, u, slot):
            order = ("q", "m", "pvT", "x")
            at = u * 4 + order.index(slot)
            while True:
                at -= 1
                pu, ps_ = at // 4, order[at % 4]
                if isinstance(it, int) and 8 * it + pu < 0:
                    return [(s["lt"], NB)]
                what = XSLOT[pu % 4][0] if ps_ == "x" else ps_
                n = a_idx(it, pu, what)
                if n is None:
                    continue
                return {"q": [(s["qs"], n + 1)], "m": [(s["mT"], n + 1)], "pvT": [(s["y"], n + 1)],
                        "kv": [(s["kpad"], n + 1), (s["kvs"], n + 1)], "v": [(s["v"], n + 1)],
                        "yT": [(s["yT"], n + 1)], "c": [(s["xo"], n + 1)]}[what]

        @block.sync
        def _(sp):
            sp.dma_start(cst[:, :], const).then_inc(ld["cst"], 16)
            sp.dma_start(wcd_s[:, :], wcd).then_inc(ld["wcd"], 16)
            sp.dma_start(wup[:, 0:D], wqu).then_inc(ld["wqu"], 16)
            sp.dma_start(wup[:, D:D + 2 * DH], wkvu).then_inc(ld["wkvu"], 16)
            sp.dma_start(wcp_s[:, :], wcp).then_inc(ld["wcp"], 16)
            sp.dma_start(wg_s[:, :], wg).then_inc(ld["wg"], 16)
            sp.dma_start(bgc[:, :], bg.rearrange("(e a) -> e a", a=1)).then_inc(ld["bg"], 16)
            sp.dma_start(xT[:, 0:NC * P].rearrange("p (e f) -> p e f", e=E), w1.rearrange("e d f -> d e f"))\
                .then_inc(ld["w1"], 16)
            sp.dma_start(xT[:, NC * P:2 * NC * P].rearrange("p (n d) -> p n d", n=NC),
                         w2.rearrange("e (c p) d -> p (e c) d", p=P)).then_inc(ld["w2"], 16)
            sp.dma_start(b1r[:, :], b1.rearrange("e (c p) -> (e c) p", p=P)).then_inc(ld["b1"], 16)
            for r in range(2):
                sp.dma_start(b2r[r * E:(r + 1) * E, :], b2).then_inc(ld["b2"], 16)
            sp.dma_start(gam[:, :], gamma.rearrange("(a d) -> a d", a=1).to_broadcast([P, D])).then_inc(ld["gam"], 16)
            sp.dma_start(bet[:, :], beta.rearrange("(a d) -> a d", a=1).to_broadcast([P, D])).then_inc(ld["bet"], 16)

            def rows(par):
                return xin[:, par, :].rearrange("p (i d) -> p i d", i=TT)

            for par in range(2):
                sp.dma_start(rows(par), seq_rows(x_v, par)).then_inc(s_x[par], 16)
            with sp.Fori(1, NB // 2) as it:
                for par in range(2):
                    sp.wait_ge(s["xn"], it * 2 + par - 1)
                    sp.dma_start(rows(par), seq_rows(x_v, it * 2 + par)).then_inc(s_x[par], 16)
            sp.wait_ge(s["xn"], NB)

            def body(it):
                for u in range(8):
                    n = a_idx(it, u, "m")
                    if n is not None:
                        r4 = a_par(u, "m") % 4
                        sp.wait_ge(s["mT"], n + 1)
                        for r in range(2):
                            sp.dma_start(qs[R_MAX + r:P:32, r4, :].bitcast(F32),
                                         ms[r * G:(r + 1) * G, a_par(u, "m") % 2, :].bitcast(F32))\
                                .then_inc(s_mrow[r4], 16)
                    if u % 4 == 2:
                        b = a_idx(it, u, "yT")
                        if b is not None:
                            par = a_par(u, "yT") % 2
                            if not (isinstance(b, int) and b < 2):
                                sp.wait_ge(s_xr[par], pair(b, it, u, "yT") * 16)
                            sp.dma_start(rows(par), seq_rows(x_v, b)).then_inc(s_xa[par], 16)
                    if u % 4 == 3:
                        b = a_idx(it, u, "c")
                        if b is not None:
                            par = a_par(u, "c") % 2
                            sp.wait_ge(s["xo"], b + 1)
                            sp.dma_start(seq_rows(resid_v, b), rows(par)).then_inc(s_xr[par], 16)
            loops(sp, body, LAGA.values(), NSTEP, 8, head=2)
            for par in range(2):
                sp.wait_ge(s_xr[par], 16 * (NB // 2))
            sp.wait_ge(s["xo"], NB)
            sp.wait_ge(s["cz"], 1)
            sp.dma_start(selcw[0:2 * E, :], selc).then_inc(ld["sel"], 16)

            def body_b(it):
                for par in range(2):
                    b = it * 2 + par
                    if not (isinstance(b, int) and b < 2):
                        sp.wait_ge(s["fo"], b - 1)
                    sp.dma_start(rows(par), seq_rows(resid_v, b)).then_inc(s_xb[par], 16)
                    if not (isinstance(b, int) and b == 0):
                        store(b - 1, (par + 1) % 2)

            def store(b, par):
                sp.wait_ge(s["fo"], b + 1)
                sp.dma_start(seq_rows(out_v, b), fo[:, par, :].rearrange("p (i d) -> p i d", i=TT))\
                    .then_inc(s_out[par], 16)
            trips(sp, body_b)
            store(NB - 1, 1)
            for par in range(2):
                sp.wait_ge(s_out[par], 16 * (NB // 2))

        @block.tensor
        def _(pe):
            def mm3(o, ah, al, bh, bl, start=True, stop=True, skip=False):
                pe.matmul(o, ah, bh, start=start, stop=False, skip_group_check=skip)
                pe.matmul(o, ah, bl, start=False, stop=False, skip_group_check=skip)
                return pe.matmul(o, al, bh, start=False, stop=stop, skip_group_check=skip)

            pe.wait_ge(ld["cst"], 16)
            pe.wait_ge(ld["wcd"], 16)
            pe.transpose(ps[0:LAT, 0, 0:P], wcd_s[:, :], ident).then_inc(s["wcdT_ps"], 1)
            pe.wait_ge(s["wcdT"], 1)
            pe.wait_ge(ld["wqu"], 16)
            pe.wait_ge(ld["wkvu"], 16)
            pe.matmul(ps[:, 1, 0:D + 2 * DH], wcdT[:, :], wup[:, :], start=True, stop=True).then_inc(s["fold_ps"], 1)
            pe.wait_ge(ld["b1"], 16)
            pe.transpose(ps[:, 2, 0:NC], b1r[:, :], ident[0:NC, 0:NC]).then_inc(s["b1_ps"], 1)
            pe.wait_ge(s["wgl"], 1)

            def body0(it):
                for u in range(2):
                    b = stage(it, u, LAG0["xT"], NB, 2)
                    if b is not None:
                        pe.wait_ge(s["xn"], b + 1)
                        if not (isinstance(it, int) and it == 0 and u == 1):
                            pe.wait_ge(s["xl0"], b)
                        for i in range(TT):
                            t = pe.transpose(ps[:, 3, bass.ts(i, P)], xn[:, (u - 1) % 2, bass.ts(i, P)], ident)
                        t.then_inc(s["xT_ps"], 1)
                    b = stage(it, u, LAG0["lg"], NB, 2)
                    if b is not None:
                        par = (u - 2) % 2
                        pe.wait_ge(s["xl0"], b + 1)
                        if not (isinstance(it, int) and 2 * it + u == 2):
                            pe.wait_ge(s["lgT"], b)
                        mm3(ps[0:E, 4, :], wgh[:, :], wgl[:, :], xh[:, par, :], xl[:, par, :]).then_inc(s["lg_ps"], 1)
                    b = stage(it, u, LAG0["lt"], NB, 2)
                    if b is not None:
                        pe.wait_ge(s["lgT"], b + 1)
                        if not (isinstance(it, int) and 2 * it + u == 3):
                            pe.wait_ge(s["lt"], b)
                        for i in range(TT):
                            t = pe.matmul(misc[:, i * E:(i + 1) * E], lgT[:, (u - 3) % 2, bass.ts(i, P)],
                                          cst[0:E, C_ID:C_ID + E], start=True, stop=True)
                        t.then_inc(s["lt_ps"], 1)
            loops(pe, body0, LAG0.values(), NB, 2, head=2)

            pe.wait_ge(s["wstl"], 1)
            pe.wait_ge(s["const_b"], 2)
            pe.wait_ge(s["kone"], 1)
            pe.wait_ge(s["vone"], 1)
            pe.wait_ge(s["w1l"], 1)
            pe.wait_ge(s["b1T"], 1)

            def misc_wait(it, u, slot):
                for sm, v in misc_freed(it, u, slot):
                    pe.wait_ge(sm, v)

            def body(it):
                for u in range(8):
                    n_mx, n_ex = a_idx(it, u, "mx"), a_idx(it, u, "ex")
                    first = isinstance(it, int) and it == 0

                    def max_unit(w):
                        if n_mx is None:
                            return
                        i, g0, gn = MX_UNITS[w]
                        cols = (i + 1) * P
                        r4, kb = a_par(u, "mx") % 4, (a_par(u, "mx") // 4) % 2
                        bank = (a_par(u, "mx") * NMX + w) % 2
                        if w == 0:
                            pe.wait_ge(s["qs"], n_mx + 1)
                        if not (first and n_mx == 0 and w < 2):
                            pe.wait_ge(s["mx"], n_mx * NMX + w - 1)
                        o = ps[:, PS_MX + bank, :]
                        if gn == 4:
                            pe.matmul(o, ident_b[:, :], causal_b[:, :], start=True, stop=False)
                            for g in range(G):
                                mm = pe.matmul(o[:, bass.ts(g, P)], qs[:, r4, 0:P], kpad[:, kb, g, 0:P],
                                               start=False, stop=(g == G - 1))
                        elif gn == 2:
                            for h in range(2):
                                mm = pe.matmul(o[:, h * cols:(h + 1) * cols], qs[:, r4, bass.ts(i, P)],
                                               kpad[:, kb, g0 + h, 0:cols], start=(h == 0), stop=False,
                                               skip_group_check=True)
                            for h in range(2):
                                mm = pe.matmul(o[:, h * cols + i * P:(h + 1) * cols], ident_b[:, :],
                                               causal_b[:, 0:P], start=False, stop=(h == 1), skip_group_check=True)
                        else:
                            pe.matmul(o[:, 0:cols], qs[:, r4, bass.ts(i, P)], kpad[:, kb, g0, 0:cols],
                                      start=True, stop=False, skip_group_check=True)
                            mm = pe.matmul(o[:, i * P:cols], ident_b[:, :], causal_b[:, 0:P],
                                           start=False, stop=True, skip_group_check=True)
                        mm.then_inc(s["mx_ps"], 1)

                    def exp_unit(w):
                        if n_ex is None:
                            return
                        i, g0 = EX_UNITS[w]
                        cols = T - i * P
                        r4, kb = a_par(u, "ex") % 4, (a_par(u, "ex") // 4) % 2
                        if w == 0:
                            pe.wait_ge(s_mrow[r4], (n_ex // 4 + 1) * 32 if isinstance(n_ex, int) else
                                       (it * 2 + a_par(u, "ex") // 4 + 1) * 32)
                        if not (first and n_ex == 0 and w < 2):
                            pe.wait_ge(s["ex"], n_ex * NEX + w - 1)
                        base = PS_EX + 2 * (w % 2)
                        if i == TT - 1:
                            pe.matmul(ps[:, base, :], ident_b[:, :], causal_t[:, :], start=True, stop=False)
                            for h in range(G):
                                mm = pe.matmul(ps[:, base, bass.ts(h, P)], kpad[:, kb, h, bass.ts(i, P)],
                                               qs[:, r4, i * P:T], start=False, stop=(h == G - 1))
                        else:
                            for h in range(EX_HEADS[w]):
                                o = ps[:, base + h, :] if EX_HEADS[w] == 2 else \
                                    ps[:, base + h // 2, (h % 2) * cols:(h % 2 + 1) * cols]
                                pe.matmul(o[:, 0:cols], kpad[:, kb, g0 + h, bass.ts(i, P)], qs[:, r4, i * P:T],
                                          start=True, stop=False, skip_group_check=True)
                                mm = pe.matmul(o[:, 0:P], ident_b[:, :], causal_t[:, 0:P], start=False, stop=True,
                                               skip_group_check=True)
                        mm.then_inc(s["ex_ps"], 1)

                    def pv(i):
                        if n_ex is None:
                            return
                        vb = (a_par(u, "ex") // 4) % 2
                        if i == 0 and not (first and n_ex == 0):
                            pe.wait_ge(s["pvs"], n_ex)
                        pe.wait_ge(s["ex"], n_ex * NEX + (2, 4, 5, 6)[i])
                        for g in range(G):
                            mm = pe.matmul(ps[32 * g:32 * g + 32, PS_PV, i * P:T], vv[:, vb, i, :],
                                           pp[:, i % 2, g, 0:T - i * P], start=(i == 0), stop=(i == TT - 1))
                        mm.then_inc(s["pv"], 1)

                    def q_proj():
                        n = a_idx(it, u, "q")
                        if n is None:
                            return
                        misc_wait(it, u, "q")
                        j, kb = a_par(u, "q") % 4, (a_par(u, "q") // 4) % 2
                        mm3(misc, wsth[:, j, :], wstl[:, j, :], xh[:, kb, :], xl[:, kb, :]).then_inc(s["q_ps"], 1)

                    def max_rows():
                        n = a_idx(it, u, "m")
                        if n is None:
                            return
                        misc_wait(it, u, "m")
                        pe.wait_ge(s["nm"], n + 1)
                        for i in range(TT):
                            t = pe.transpose(misc[0:2 * G, bass.ts(i, P)],
                                             nmhl[:, a_par(u, "m") % 2, i, :, :].rearrange("p r g -> p (r g)"), ident)
                        t.then_inc(s["mT_ps"], 1)

                    def pv_turn():
                        n = a_idx(it, u, "pvT")
                        if n is None:
                            return
                        misc_wait(it, u, "pvT")
                        pe.wait_ge(s["pvs"], n + 1)
                        for i in range(TT):
                            t = pe.transpose(misc[:, bass.ts(i, P)], pvs[:, bass.ts(i, P)], ident)
                        t.then_inc(s["pvT_ps"], 1)

                    def extra():
                        what, _ = XSLOT[u % 4]
                        n = a_idx(it, u, what)
                        if n is None:
                            return
                        misc_wait(it, u, "x")
                        par = a_par(u, what) % 2
                        if what == "kv":
                            pe.wait_ge(s["xl"], n + 1)
                            mm3(misc, wsth[:, NJ, :], wstl[:, NJ, :], xh[:, par, :], xl[:, par, :])\
                                .then_inc(s["kv_ps"], 1)
                        elif what == "v":
                            pe.wait_ge(s["kvs"], n + 1)
                            for i in range(TT):
                                t = pe.transpose(misc[:, bass.ts(i, P)], kvs[:, bass.ts(i, P)], ident)
                            t.then_inc(s["v_ps"], 1)
                        elif what == "yT":
                            for i in range(TT):
                                t = pe.transpose(misc[:, bass.ts(i, P)], y[:, par, i, :], ident)
                            t.then_inc(s["yT_ps"], 1)
                        else:
                            pe.wait_ge(s["yT"], n + 1)
                            for i in range(TT):
                                t = pe.matmul(misc[:, bass.ts(i, P)], yT[:, bass.ts(i, P)], wcp_s[:, :],
                                              start=True, stop=True)
                            t.then_inc(s["c_ps"], 1)

                    max_unit(0)
                    max_unit(1)
                    q_proj()
                    exp_unit(0)
                    exp_unit(1)
                    max_unit(2)
                    max_unit(3)
                    max_rows()
                    exp_unit(2)
                    pv(0)
                    max_unit(4)
                    pv_turn()
                    exp_unit(3)
                    max_unit(5)
                    exp_unit(4)
                    pv(1)
                    max_unit(6)
                    extra()
                    exp_unit(5)
                    max_unit(7)
                    pv(2)
                    max_unit(8)
                    max_unit(9)
                    pv(3)
                    max_unit(10)
            loops(pe, body, LAGA.values(), NSTEP, 8)

            pe.wait_ge(s["selr"], 1)
            pe.wait_ge(s["w2l"], 1)
            pe.wait_ge(s["b2l"], 1)

            def turn_out(b):
                pe.wait_ge(s["fadd"], (b + 1) * (E - 1))
                if not (isinstance(b, int) and b == 0):
                    pe.wait_ge(s["fz"], b)
                for i in range(TT):
                    o = misc[:, bass.ts(i, P)]
                    pe.matmul(o, cws[0:2 * E, bass.ts(i, P)], b2h[:, :], start=True, stop=False)
                    pe.matmul(o, cws[0:2 * E, bass.ts(i, P)], b2l[:, :], start=False, stop=False)
                    t = pe.matmul(o, facc[:, bass.ts(i, P)], ident, start=False, stop=True)
                t.then_inc(s["ft_ps"], 1)

            def body_b(it):
                for par in range(2):
                    b = it * 2 + par
                    first = isinstance(b, int) and b == 0
                    for c in range(NC + LW2):
                        if c < NC:
                            if c == 0:
                                pe.wait_ge(s["zl"], b + 1)
                            if not (first and c < 4):
                                pe.wait_ge(s["hf"], b * NC + c - 3)
                            mm3(ps[:, c % 4, :], w1h[:, bass.ts(c, P)], w1l[:, bass.ts(c, P)],
                                zh[:, par, :], zl[:, par, :]).then_inc(s["h_ps"], 1)
                        if c == 2:
                            if not first:
                                turn_out(b - 1)
                            pe.wait_ge(s["cwst"], b + 1)
                            if not first:
                                pe.wait_ge(s["cwb"], b * E)
                            for i in range(TT):
                                t = pe.transpose(ps[0:2 * E, 6, bass.ts(i, P)], cwst[:, bass.ts(i, 2 * E)], ident)
                            t.then_inc(s["ct_ps"], 1)
                        e = c // FC - 1
                        if c >= FC and c % FC == 0:
                            if e == 0:
                                pe.wait_ge(s["cws"], b + 1)
                            else:
                                pe.wait_ge(s["cwb"], b * E + e)
                            pe.matmul(ps[:, 6, :], selr[:, bass.ts(e, P)], cws[:, :], start=True, stop=True)\
                                .then_inc(s["cb_ps"], 1)
                        if c >= LW2:
                            c2 = c - LW2
                            e2, k = c2 // FC, c2 % FC
                            if k == 0 and not (first and e2 < 2):
                                pe.wait_ge(s["yw"], b * E + e2 - 1)
                            pe.wait_ge(s["hl"], b * NC + c2 + 1)
                            mm = mm3(ps[:, 4 + e2 % 2, :], w2h[:, bass.ts(c2, P)], w2l[:, bass.ts(c2, P)],
                                     hh[:, c2 % 4, :], hl[:, c2 % 4, :], start=(k == 0), stop=(k == FC - 1))
                            mm.then_inc(s["y_ps"], 1)
            trips(pe, body_b)
            turn_out(NB - 1)

        @block.scalar
        def _(act):
            def copy(o, i):
                return act.activation(o, i, ACT.Copy)

            act.wait_ge(ld["cst"], 16)
            for r in range(4):
                copy(causal_b[:, bass.ts(r, P)], cst[:, C_CAUSAL:C_CAUSAL + P])
            for r in range(4):
                t = copy(causal_t[:, bass.ts(r, P)], cst[:, C_CAUSALT:C_CAUSALT + P])
            t.then_inc(s["const_b"], 1)
            copy(ident_b[:, :], ident).then_inc(s["const_b"], 1)
            act.wait_ge(s["wcdT_ps"], 1)
            copy(wcdT[:, :], ps[0:LAT, 0, 0:P]).then_inc(s["wcdT"], 1)
            act.wait_ge(s["fold_ps"], 1)
            copy(wfold[:, :], ps[:, 1, 0:D + 2 * DH]).then_inc(s["fold"], 1)
            act.wait_ge(s["b1_ps"], 1)
            copy(b1T[:, :], ps[:, 2, 0:NC]).then_inc(s["b1T"], 1)
            act.wait_ge(ld["wg"], 16)
            copy(wgh[:, :], wg_s[:, :]).then_inc(s["wgh"], 1)
            act.wait_ge(ld["b2"], 32)
            copy(b2h[:, :], b2r[:, :]).then_inc(s["b2h"], 1)
            act.wait_ge(s["wst"], 1)
            copy(wsth[:, :, :], wst[:, :, :]).then_inc(s["wsth"], 1)
            act.wait_ge(ld["w1"], 16)
            copy(w1h[:, :], xT[:, 0:NC * P]).then_inc(s["w1h"], 1)
            act.wait_ge(ld["w2"], 16)
            copy(w2h[:, :], xT[:, NC * P:2 * NC * P]).then_inc(s["w2h"], 1)
            act.wait_ge(s["w2l"], 1)
            act.wait_ge(ld["bg"], 16)

            def body0(it):
                for u in range(2):
                    b = stage(it, u, LAG0["xT"], NB, 2)
                    if b is not None:
                        par = (u - 1) % 2
                        act.wait_ge(s["xT_ps"], b + 1)
                        if not (isinstance(it, int) and 2 * it + u < 3):
                            act.wait_ge(s["lg_ps"], b - 1)
                        copy(xh[:, par, :], ps[:, 3, :]).then_inc(s["xh0"], 1)
                        copy(xT[:, bass.ts(b, T)], ps[:, 3, :]).then_inc(s["xT"], 1)
                    b = stage(it, u, LAG0["lg"], NB, 2)
                    if b is not None:
                        par = (u - 2) % 2
                        act.wait_ge(s["lg_ps"], b + 1)
                        if not (isinstance(it, int) and 2 * it + u < 4):
                            act.wait_ge(s["lt_ps"], b - 1)
                        act.activation(lgT[:, par, :], ps[0:E, 4, :], ACT.Identity, bias=bgc[:, :])\
                            .then_inc(s["lgT"], 1)
            loops(act, body0, LAG0.values(), NB, 2, head=2)
            act.wait_ge(s["rt"], 3)
            act.activation(w_r[:, :, :], w_r[:, :, :], ACT.Exp).then_inc(s["rexp"], 1)

            def body(it):
                for u in range(8):
                    n = a_idx(it, u, "pvT")
                    n_ex = a_idx(it, u, "ex")
                    first = isinstance(it, int) and it == 0
                    if u % 4 == 0:
                        b = a_idx(it, u, "kv")
                        if b is not None:
                            if not (isinstance(b, int) and b < 2):
                                act.wait_ge(s["q_ps"], 4 * b - 4)
                            else:
                                act.wait_ge(s["lg_ps"], NB)
                            act.wait_ge(s["xT"], NB)
                            copy(xh[:, a_par(u, "kv") % 2, :], xT[:, bass.ts(b, T)]).then_inc(s["xh"], 1)
                    if n is not None:
                        act.wait_ge(s["pv"], (n + 1) * TT)
                        if not (isinstance(n, int) and n == 0):
                            act.wait_ge(s["pvT_ps"], n)
                        copy(pvs[:, :], ps[:, PS_PV, :]).then_inc(s["pvs"], 1)
                    n = a_idx(it, u, "q")
                    if n is not None:
                        act.wait_ge(s["q_ps"], n + 1)
                        if not (isinstance(n, int) and n < 2):
                            act.wait_ge(s["qs"], n - 1)
                        copy(qh[:, a_par(u, "q") % 2, :], misc).then_inc(s["qh"], 1)

                    def exp_unit(w):
                        if n_ex is None:
                            return
                        i, g0 = EX_UNITS[w]
                        cols = T - i * P
                        act.wait_ge(s["ex_ps"], n_ex * NEX + w + 1)
                        if g0 == 0 and not (first and n_ex == 0 and i < 2):
                            act.wait_ge(s["pv"], n_ex * TT + i - 1)
                        base = PS_EX + 2 * (w % 2)
                        if EX_HEADS[w] == 2:
                            o = pp[:, i % 2, g0:g0 + 2, 0:cols]
                            a = ps[:, base:base + 2, 0:cols]
                        elif i == 2:
                            o = pp[:, 0, :, 0:cols].rearrange("p (a b) c -> p a b c", a=2)
                            a = ps[:, base:base + 2, :].rearrange("p a (b c) -> p a b c", b=2)
                        else:
                            o = pp[:, 1, :, 0:cols]
                            a = ps[:, base, :].rearrange("p (b c) -> p b c", b=G)
                        act.activation(o, a, ACT.Exp, scale=SCALE).then_inc(s["ex"], 1)

                    exp_unit(0)
                    exp_unit(1)
                    n = a_idx(it, u, "m")
                    if n is not None:
                        act.wait_ge(s["mT_ps"], n + 1)
                        if not (isinstance(n, int) and n < 2):
                            r4 = (a_par(u, "m") - 2) % 4
                            act.wait_ge(s_mrow[r4], (n - 2) // 4 * 32 + 32 if isinstance(n, int) else
                                        (it * 2 + (a_par(u, "m") - 2) // 4 + 1) * 32)
                        copy(ms[:, a_par(u, "m") % 2, :], misc[0:2 * G, :]).then_inc(s["mT"], 1)
                    exp_unit(2)
                    exp_unit(3)
                    exp_unit(4)
                    what, _ = XSLOT[u % 4]
                    n = a_idx(it, u, what)
                    if n is not None:
                        par = a_par(u, what) % 2
                        if what == "kv":
                            act.wait_ge(s["kv_ps"], n + 1)
                            if not (isinstance(n, int) and n == 0):
                                act.wait_ge(s["kpad"], n)
                                act.wait_ge(s["v_ps"], n)
                            copy(kh[:, :], misc).then_inc(s["kh"], 1)
                            copy(kvs[:, :], misc).then_inc(s["kvs"], 1)
                        elif what == "v":
                            act.wait_ge(s["v_ps"], n + 1)
                            if not (isinstance(n, int) and n < 2):
                                act.wait_ge(s["pv"], (4 * n - 4) * TT)
                            copy(vv[:, par, :, 0:DH], misc.rearrange("p (i c) -> p i c", i=TT)
                                 [:, :, R_MAX:R_MAX + DH]).then_inc(s["v"], 1)
                        elif what == "yT":
                            act.wait_ge(s["yT_ps"], n + 1)
                            if not (isinstance(n, int) and n == 0):
                                act.wait_ge(s["c_ps"], n)
                            copy(yT[:, :], misc).then_inc(s["yT"], 1)
                    exp_unit(5)
            loops(act, body, LAGA.values(), NSTEP, 8, head=2)

            act.wait_ge(s["xo"], NB)
            act.wait_ge(ld["sel"], 16)
            copy(selr[:, :], selcw[:, :]).then_inc(s["selr"], 1)

            def split_x(b, par, first):
                if not first:
                    act.wait_ge(s["h_ps"], (b - 1) * NC)
                copy(zh[:, par, :], xT[:, bass.ts(b, T)]).then_inc(s["zh"], 1)
            split_x(0, 0, True)

            def body_b(it):
                for par in range(2):
                    b = it * 2 + par
                    first = isinstance(b, int) and b == 0
                    if first:
                        act.wait_ge(s["cw"], 1)
                    else:
                        act.wait_ge(s["ct_ps"], b)
                    copy(cwst[:, :], cwhl[:, bass.ts(b, TT), :].rearrange("p i r -> p (i r)"))\
                        .then_inc(s["cwst"], 1)
                    for c in range(NC):
                        act.wait_ge(s["h_ps"], b * NC + c + 1)
                        if not (first and c < 4):
                            act.wait_ge(s["hl"], b * NC + c - 3)
                        act.activation(hf[:, c % 4, :], ps[:, c % 4, :], ACT.Gelu, bias=b1T[:, c:c + 1])\
                            .then_inc(s["hf"], 1)
                        if c % 2:
                            act.wait_ge(s["hf"], b * NC + c + 1)
                            if not (first and c < 4):
                                act.wait_ge(s["y_ps"], b * NC + c - 3)
                            copy(hh[:, c % 4, :], hf[:, c % 4, :]).then_inc(s["hh_a"], 1)
                        if c == 2:
                            act.wait_ge(s["ct_ps"], b + 1)
                            if not first:
                                act.wait_ge(s["ft_ps"], b)
                            else:
                                act.wait_ge(s["cz"], 2)
                            copy(cws[0:2 * E, :], ps[0:2 * E, 6, :]).then_inc(s["cws"], 1)
                        e = c // FC - 1
                        if c >= FC and c % FC == 0 or c == NC - 1:
                            if c == NC - 1:
                                e = E - 1
                            act.wait_ge(s["cb_ps"], b * E + e + 1)
                            if not (first and e < 2):
                                act.wait_ge(s["yw"], b * E + e - 1)
                            copy(cwb[:, e % 2, :], ps[:, 6, :]).then_inc(s["cwb"], 1)
                        if c == NC // 2 and not (isinstance(b, int) and b == NB - 1):
                            split_x(b + 1, (par + 1) % 2, first)
            trips(act, body_b)

        @block.vector
        def _(dve):
            negq = cst[:, C_NEGQ:C_NEGQ + 1]
            negk = cst[:, C_NEGK:C_NEGK + 1]
            dve.memset(kpad[:, :, :, :].rearrange("p a g t -> p (a g t)").bitcast(F32), 0.0).then_inc(s["kz"], 1)
            dve.memset(wst[:, :, :], 0.0).then_inc(s["wst0"], 1)
            dve.wait_ge(ld["cst"], 16)
            dve.wait_ge(s["kz"], 1)
            for par in range(2):
                for g in range(G):
                    o = kpad[32 * g:32 * g + 32, par, g, :]
                    t = dve.tensor_scalar(o, o.bitcast(F32), cst[32 * g:32 * g + 32, C_ONEK:C_ONEK + 1], None, ALU.add)
            t.then_inc(s["kone"], 1)
            dve.wait_ge(s["fold"], 1)
            dve.wait_ge(s["wst0"], 1)
            for r in range(3):
                dve.tensor_copy(wst[:, 0:NJ, :].rearrange("p j (g c) -> p (j g) c", g=G)[:, :, r * DH:(r + 1) * DH],
                                wfold[:, 0:D].rearrange("p (h c) -> p h c", h=H))
                for g in range(G):
                    dve.tensor_copy(wst[:, NJ, 32 * g + r * DH:32 * g + (r + 1) * DH], wfold[:, D:D + DH])
            for g in range(G):
                t = dve.tensor_copy(wst[:, NJ, 32 * g + R_MAX:32 * g + R_MAX + DH], wfold[:, D + DH:D + 2 * DH])
            t.then_inc(s["wst"], 1)
            dve.wait_ge(s["wgh"], 1)
            dve.tensor_tensor(wgl[:, :], wg_s[:, :], wgh[:, :].bitcast(F32), ALU.subtract).then_inc(s["wgl"], 1)
            dve.wait_ge(s["b2h"], 1)
            dve.tensor_tensor(b2l[:, :], b2r[:, :], b2h[:, :].bitcast(F32), ALU.subtract).then_inc(s["b2l"], 1)
            dve.wait_ge(s["wsth"], 1)
            dve.wait_ge(s["wst"], 1)
            dve.tensor_tensor(wstl[:, :, :], wst[:, :, :], wsth[:, :, :].bitcast(F32), ALU.subtract)\
                .then_inc(s["wstl"], 1)
            dve.wait_ge(s["w1h"], 1)
            dve.tensor_tensor(w1l[:, :], xT[:, 0:NC * P], w1h[:, :].bitcast(F32), ALU.subtract).then_inc(s["w1l"], 1)
            dve.wait_ge(s["w2h"], 1)
            dve.tensor_tensor(w2l[:, :], xT[:, NC * P:2 * NC * P], w2h[:, :].bitcast(F32), ALU.subtract)\
                .then_inc(s["w2l"], 1)

            def body0(it):
                for u in range(2):
                    b = stage(it, u, LAG0["x"], NB, 2)
                    if b is not None:
                        dve.wait_ge(s_x[u], (it + 1) * 16)
                        if not (isinstance(it, int) and it == 0):
                            dve.wait_ge(s["xn"], b - 1)
                        for i in range(TT):
                            t = dve.bn_stats(stats[:, u, i, :], xin[:, u, bass.ts(i, D)])
                        t.then_inc(s["stat"], 1)
                        dve.wait_ge(s["stat"], b + 1)
                        plain(dve)
                        for i in range(TT):
                            t = dve.bn_aggr(mv[:, u, i, :], stats[:, u, i, :])
                        t.then_inc(s["mv"], 1)
                    b = stage(it, u, LAG0["xT"], NB, 2)
                    if b is not None:
                        par = (u - 1) % 2
                        dve.wait_ge(s["rstd"], b + 1)
                        dve.wait_ge(s["mv"], b + 1)
                        if not (isinstance(it, int) and 2 * it + u < 3):
                            dve.wait_ge(s["xT_ps"], b - 1)
                        for i in range(TT):
                            t = dve.tensor_scalar(xn[:, par, bass.ts(i, D)], xin[:, par, bass.ts(i, D)],
                                                  mv[:, par, i, 0:1], rstd[:, par, i:i + 1], ALU.subtract, ALU.mult)
                        t.then_inc(s["xn"], 1)
                        dve.wait_ge(s["xT"], b + 1)
                        dve.wait_ge(s["xh0"], b + 1)
                        if not (isinstance(it, int) and 2 * it + u < 3):
                            dve.wait_ge(s["lg_ps"], b - 1)
                        dve.tensor_tensor(xl[:, par, :], ps[:, 3, :], xh[:, par, :].bitcast(F32), ALU.subtract)\
                            .then_inc(s["xl0"], 1)
                    b = stage(it, u, LAG0["lt"], NB, 2)
                    if b is not None:
                        dve.wait_ge(s["lt_ps"], b + 1)
                        dve.tensor_copy(w_r[:, bass.ts(b, TT), :], misc[:, 0:TT * E].rearrange("p (i e) -> p i e", i=TT))\
                            .then_inc(s["lt"], 1)
            loops(dve, body0, LAG0.values(), NB, 2, head=2)

            wide = lambda a: a.rearrange("p (t a) -> p t a", a=1).to_broadcast([P, NT, E])
            dve.wait_ge(s["lt"], NB)
            dve.tensor_reduce(rsm[:, :], w_r[:, :, :], AX_X, ALU.max).then_inc(s["rt"], 1)
            dve.wait_ge(s["rt"], 1)
            dve.tensor_tensor(w_r[:, :, :], w_r[:, :, :], wide(rsm[:, :]), ALU.subtract).then_inc(s["rt"], 2)
            dve.wait_ge(s["rexp"], 1)
            dve.tensor_reduce(rsm[:, :], w_r[:, :, :], AX_X, ALU.add).then_inc(s["rt"], 1)
            dve.wait_ge(s["rt"], 4)
            dve.reciprocal(rsr[:, :], rsm[:, :]).then_inc(s["rt"], 1)
            dve.wait_ge(s["rt"], 5)
            dve.tensor_tensor(w_r[:, :, :], w_r[:, :, :], wide(rsr[:, :]), ALU.mult).then_inc(s["rt"], 1)
            dve.wait_ge(s["rt"], 6)
            done = 6
            NH = NT // 2
            for h in range(2):
                ca = cmpa.rearrange("p (t e f) -> p t e f", e=E, f=E)
                cb = cmpb.rearrange("p (t e f) -> p t e f", e=E, f=E)
                wv = w_r[:, h * NH:(h + 1) * NH, :]
                other = wv.rearrange("p t (a f) -> p t a f", a=1).to_broadcast([P, NH, E, E])
                own = wv.rearrange("p t (e a) -> p t e a", a=1).to_broadcast([P, NH, E, E])
                dve.tensor_tensor(ca, other, own, ALU.is_gt)
                dve.tensor_tensor(cb, other, own, ALU.is_equal).then_inc(s["rt"], 1)
                dve.wait_ge(s["rt"], done + 1)
                less = cst[:, C_LESS:C_LESS + E * E].rearrange("p (a e f) -> p a e f", a=1, f=E)\
                    .to_broadcast([P, NH, E, E])
                dve.tensor_tensor(cb, cb, less, ALU.mult).then_inc(s["rt"], 1)
                dve.wait_ge(s["rt"], done + 2)
                dve.tensor_tensor(ca, ca, cb, ALU.add).then_inc(s["rt"], 1)
                dve.wait_ge(s["rt"], done + 3)
                dve.tensor_reduce(rank[:, h * NH:(h + 1) * NH, :], ca, AX_X, ALU.add).then_inc(s["rt"], 1)
                dve.wait_ge(s["rt"], done + 4)
                done += 4
            dve.tensor_scalar(rank[:, :, :], rank[:, :, :], 2.0, None, ALU.is_lt).then_inc(s["rt"], 1)
            dve.wait_ge(s["rt"], done + 1)
            dve.tensor_tensor(w_c[:, :, :], rank[:, :, :], w_r[:, :, :], ALU.mult).then_inc(s["rt"], 1)
            dve.wait_ge(s["rt"], done + 2)
            dve.tensor_reduce(rsm[:, :], w_c[:, :, :], AX_X, ALU.add).then_inc(s["rt"], 1)
            dve.wait_ge(s["rt"], done + 3)
            dve.tensor_scalar(rsm[:, :], rsm[:, :], EPS_GATE, None, ALU.add).then_inc(s["rt"], 1)
            dve.wait_ge(s["rt"], done + 4)
            dve.reciprocal(rsr[:, :], rsm[:, :]).then_inc(s["rt"], 1)
            dve.wait_ge(s["rt"], done + 5)
            dve.tensor_tensor(w_c[:, :, :], w_c[:, :, :], wide(rsr[:, :]), ALU.mult).then_inc(s["rt"], 1)
            dve.wait_ge(s["rt"], done + 6)
            dve.tensor_copy(cwh_r[:, :, :], w_c[:, :, :]).then_inc(s["rt"], 1)
            dve.wait_ge(s["rt"], done + 7)
            dve.tensor_copy(cwhl[:, :, 0:E], cwh_r[:, :, :].bitcast(F32))
            dve.tensor_tensor(cwhl[:, :, E:2 * E], w_c[:, :, :], cwh_r[:, :, :].bitcast(F32), ALU.subtract)\
                .then_inc(s["cw"], 1)

            def body(it):
                for u in range(8):
                    n_mx = a_idx(it, u, "mx")
                    if u % 4 == 0:
                        b = a_idx(it, u, "kv")
                        if b is not None:
                            dve.wait_ge(s["xh"], b + 1)
                            par = a_par(u, "kv") % 2
                            dve.tensor_tensor(xl[:, par, :], xT[:, bass.ts(b, T)], xh[:, par, :].bitcast(F32),
                                              ALU.subtract).then_inc(s["xl"], 1)

                    def reduce(w):
                        if n_mx is None:
                            return
                        i, g0, gn = MX_UNITS[w]
                        cols = (i + 1) * P
                        bank = (a_par(u, "mx") * NMX + w) % 2
                        dve.wait_ge(s["mx_ps"], n_mx * NMX + w + 1)
                        if w == 0 and not (isinstance(n_mx, int) and n_mx == 0):
                            dve.wait_ge(s["nm"], n_mx)
                        dve.tensor_reduce(nm[:, i, g0:g0 + gn],
                                          ps[:, PS_MX + bank, 0:gn * cols].rearrange("p (g c) -> p g c", g=gn),
                                          AX_X, ALU.max, negate=True).then_inc(s["mx"], 1)

                    reduce(0)
                    reduce(1)
                    n = a_idx(it, u, "q")
                    if n is not None:
                        par = a_par(u, "q")
                        dve.wait_ge(s["qh"], n + 1)
                        if not (isinstance(n, int) and n < 4):
                            dve.wait_ge(s["ex_ps"], (n - 3) * NEX)
                        dve.scalar_tensor_tensor(out=qs[:, par % 4, :], in0=qh[:, par % 2, :].bitcast(F32), scalar=negq,
                                                 in1=misc, op0=ALU.mult, op1=ALU.add).then_inc(s["qs"], 1)
                    reduce(2)
                    reduce(3)
                    reduce(4)
                    n = a_idx(it, u, "pvT")
                    if n is not None:
                        par = a_par(u, "pvT")
                        dve.wait_ge(s["pvT_ps"], n + 1)
                        sums = misc.rearrange("p (n c) -> p n c", c=32)
                        dve.reciprocal(rden[:, :].rearrange("p (n a) -> p n a", a=1), sums[:, :, DH:DH + 1])\
                            .then_inc(s["rden"], 1)
                        dve.wait_ge(s["rden"], n + 1)
                        if par % 4 == 0 and not (isinstance(n, int) and n < 8):
                            dve.wait_ge(s["yT_ps"], (n if isinstance(n, int) else 0) // 4 - 1 if isinstance(n, int)
                                        else it * 2 + par // 4 - 1)
                        j = par % 4
                        dve.tensor_tensor(
                            y[:, (par // 4) % 2, :, j * G * DH:(j + 1) * G * DH].rearrange("p i (g c) -> p i g c", g=G),
                            misc.rearrange("p (i g c) -> p i g c", i=TT, g=G)[:, :, :, 0:DH],
                            rden[:, :].rearrange("p (i g a) -> p i g a", i=TT, a=1).to_broadcast([P, TT, G, DH]),
                            ALU.mult).then_inc(s["y"], 1)
                    reduce(5)
                    reduce(6)
                    what, _ = XSLOT[u % 4]
                    n = a_idx(it, u, what)
                    if n is not None and what == "kv":
                        dve.wait_ge(s["kh"], n + 1)
                        dve.wait_ge(s["kvs"], n + 1)
                        par = a_par(u, what) % 2
                        if not (isinstance(n, int) and n < 2):
                            dve.wait_ge(s["ex_ps"], (4 * n - 4) * NEX)
                        else:
                            dve.wait_ge(s["kone"], 1)
                        for g in range(G):
                            r = slice(32 * g, 32 * g + R_MAX)
                            t = dve.scalar_tensor_tensor(out=kpad[r, par, g, :], in0=kh[r, :].bitcast(F32),
                                                         scalar=negk[r, :], in1=misc[r, :], op0=ALU.mult, op1=ALU.add)
                        t.then_inc(s["kpad"], 1)
                    if n is not None and what == "c":
                        dve.wait_ge(s["c_ps"], n + 1)
                        par = a_par(u, what) % 2
                        dve.wait_ge(s_xa[par], (pair(n, it, u, what) + 1) * 16)
                        xb = xin[:, par, :]
                        dve.tensor_tensor(xb, xb, misc, ALU.add).then_inc(s["xo"], 1)
                    for w in range(7, NMX):
                        reduce(w)
                    if n_mx is not None:
                        par = a_par(u, "mx") % 2
                        dve.wait_ge(s["mx"], (n_mx + 1) * NMX)
                        dve.tensor_copy(nmh_r[:, :, :], nm[:, :, :]).then_inc(s["nm1"], 1)
                        dve.wait_ge(s["nm1"], n_mx + 1)
                        if not (isinstance(n_mx, int) and n_mx < 2):
                            dve.wait_ge(s["mT_ps"], n_mx - 1)
                        dve.tensor_copy(nmhl[:, par, :, 0, :], nmh_r[:, :, :].bitcast(F32))
                        dve.tensor_tensor(nmhl[:, par, :, 1, :], nm[:, :, :], nmh_r[:, :, :].bitcast(F32), ALU.subtract)\
                            .then_inc(s["nm"], 1)
            loops(dve, body, LAGA.values(), NSTEP, 8, head=2)

            dve.wait_ge(s["c_ps"], NB)
            dve.wait_ge(s["xo"], NB)
            dve.memset(selcw[:, :], 0.0).then_inc(s["cz"], 1)
            dve.memset(cws[:, :].bitcast(F32), 0.0).then_inc(s["cz"], 1)

            def split_x(b, par):
                dve.wait_ge(s["zh"], b + 1)
                dve.tensor_tensor(zl[:, par, :], xT[:, bass.ts(b, T)], zh[:, par, :].bitcast(F32), ALU.subtract)\
                    .then_inc(s["zl"], 1)
            split_x(0, 0)

            def weigh(b, e, first):
                dve.wait_ge(s["y_ps"], b * NC + (e + 1) * FC)
                dve.wait_ge(s["cwb"], b * E + e + 1)
                if e == 0:
                    if not first:
                        dve.wait_ge(s["ft_ps"], b)
                    o = facc[:, :]
                else:
                    if not (first and e < 3):
                        dve.wait_ge(s["fadd"], b * (E - 1) + max(e - 2, 0))
                    o = yw[:, e % 2, :]
                dve.tensor_tensor(o, ps[:, 4 + e % 2, :], cwb[:, e % 2, :], ALU.mult).then_inc(s["yw"], 1)

            def out_stats(b):
                dve.wait_ge(s["ft_ps"], b + 1)
                if not (isinstance(b, int) and b == 0):
                    dve.wait_ge(s["fz"], b)
                for i in range(TT):
                    t = dve.bn_stats(fst[:, i, :], misc[:, bass.ts(i, D)])
                t.then_inc(s["fst"], 1)
                dve.wait_ge(s["fst"], b + 1)
                plain(dve)
                for i in range(TT):
                    t = dve.bn_aggr(fmv[:, i, :], fst[:, i, :])
                t.then_inc(s["fmv"], 1)

            def out_norm(b):
                dve.wait_ge(s["frs"], b + 1)
                dve.wait_ge(s["fmv"], b + 1)
                if not (isinstance(b, int) and b == 0):
                    dve.wait_ge(s["fo"], b)
                for i in range(TT):
                    t = dve.tensor_scalar(fz[:, bass.ts(i, D)], misc[:, bass.ts(i, D)], fmv[:, i, 0:1],
                                          frs[:, i:i + 1], ALU.subtract, ALU.mult)
                t.then_inc(s["fz"], 1)

            def body_b(it):
                for par in range(2):
                    b = it * 2 + par
                    first = isinstance(b, int) and b == 0
                    for c in range(NC):
                        dve.wait_ge(s["hf"], b * NC + c + 1)
                        if not (first and c < 4):
                            dve.wait_ge(s["y_ps"], b * NC + c - 3)
                        if c % 2 == 0:
                            dve.tensor_copy(hh[:, c % 4, :], hf[:, c % 4, :]).then_inc(s["hh_d"], 1)
                            dve.wait_ge(s["hh_d"], b * (NC // 2) + c // 2 + 1)
                        else:
                            dve.wait_ge(s["hh_a"], b * (NC // 2) + c // 2 + 1)
                        dve.tensor_tensor(hl[:, c % 4, :], hf[:, c % 4, :], hh[:, c % 4, :].bitcast(F32), ALU.subtract)\
                            .then_inc(s["hl"], 1)
                        if c % FC == 1 and c > FC:
                            weigh(b, (c - 5) // FC, first)
                        if c == 3 and not first:
                            out_stats(b - 1)
                        if c == 6 and not first:
                            out_norm(b - 1)
                        if c == NC // 2 + 2 and not (isinstance(b, int) and b == NB - 1):
                            split_x(b + 1, (par + 1) % 2)
                    weigh(b, E - 1, first)
            trips(dve, body_b)
            out_stats(NB - 1)
            out_norm(NB - 1)

        @block.gpsimd
        def _(pool):
            half = cst[:, C_HALF:C_HALF + TT]
            pool.memset(vv[:, :, :, :], 0.0).then_inc(s["vz"], 1)
            pool.wait_ge(s["vz"], 1)
            pool.memset(vv[:, :, :, DH:DH + 1], 1.0).then_inc(s["vone"], 1)
            pool.wait_ge(ld["cst"], 16)

            def body0(it):
                for u in range(2):
                    b = stage(it, u, LAG0["x"], NB, 2)
                    if b is None:
                        continue
                    pool.wait_ge(s["mv"], b + 1)
                    if not (isinstance(it, int) and it == 0):
                        pool.wait_ge(s["xn"], b - 1)
                    plain(pool)
                    pool.tensor_scalar(veps[:, u, :], mv[:, u, :, 1], EPS_LN, None, ALU.add).then_inc(s["veps"], 1)
                    pool.wait_ge(s["veps"], b + 1)
                    pool.tensor_tensor(rstd[:, u, :], veps[:, u, :], half, ALU.pow).then_inc(s["rstd"], 1)
            body0(0)
            with pool.Fori(1, NB // 2) as it:
                body0(it)


            pool.wait_ge(s["xo"], NB)
            pool.wait_ge(ld["gam"], 16)
            pool.wait_ge(ld["bet"], 16)

            def finish(b, par, stored_before):
                pool.wait_ge(s["fmv"], b + 1)
                plain(pool)
                pool.tensor_scalar(fve[:, :], fmv[:, :, 1], EPS_LN, None, ALU.add).then_inc(s["fve"], 1)
                pool.wait_ge(s["fve"], b + 1)
                if not (isinstance(b, int) and b == 0):
                    pool.wait_ge(s["fz"], b)
                pool.tensor_tensor(frs[:, :], fve[:, :], half, ALU.pow).then_inc(s["frs"], 1)
                row = lambda a: a.rearrange("p (i d) -> p i d", i=TT)
                over = lambda a: a.rearrange("p (i d) -> p i d", i=1).to_broadcast([P, TT, D])
                pool.wait_ge(s["fz"], b + 1)
                o = row(fo[:, par, :])
                if not (isinstance(b, int) and b < 2):
                    pool.wait_ge(s_out[par], stored_before)
                pool.tensor_tensor(o, row(fz[:, :]), over(gam[:, :]), ALU.mult).then_inc(s["fg"], 1)
                pool.wait_ge(s["fg"], b + 1)
                pool.tensor_tensor(o, o, over(bet[:, :]), ALU.add).then_inc(s["fb"], 1)
                pool.wait_ge(s["fb"], b + 1)
                pool.wait_ge(s_xb[par], stored_before + 16)
                pool.tensor_tensor(o, o, row(xin[:, par, :]), ALU.add).then_inc(s["fo"], 1)

            def body_b(it):
                for par in range(2):
                    b = it * 2 + par
                    first = isinstance(b, int) and b == 0
                    if not first:
                        finish(b - 1, (par + 1) % 2, (it - 1 + par) * 16)
                    for e in range(1, E):
                        pool.wait_ge(s["yw"], b * E + e + 1)
                        if not (first and e == 1):
                            pool.wait_ge(s["fadd"], b * (E - 1) + e - 1)
                        pool.tensor_tensor(facc[:, :], facc[:, :], yw[:, e % 2, :], ALU.add).then_inc(s["fadd"], 1)
            trips(pool, body_b, 2)
            finish(NB - 1, 1, (NB // 2 - 1) * 16)


_INS = ["L0_attn_x", "L0_attn_Wc_down", "L0_attn_Wq_up", "L0_attn_Wkv_up", "L0_attn_Wc_proj", "L0_ffn_Wg",
        "L0_ffn_bg", "L0_ffn_W1", "L0_ffn_b1", "L0_ffn_W2", "L0_ffn_b2", "L0_ffn_gamma", "L0_ffn_beta"]


def kernel(**inputs):
    import numpy as _np
    import concourse.bacc as _bacc
    from concourse import mybir as _mybir
    from concourse.bass_utils import run_bass_kernel_spmd as _run

    const = _np.zeros((P, C_END), _np.float32)
    row = _np.arange(P)
    const[:, C_ID:C_ID + P] = _np.eye(P)
    const[:, C_CAUSAL:C_CAUSAL + P] = _np.where(row[None, :] <= row[:, None], 0.0, -1e30)
    const[:, C_CAUSALT:C_CAUSALT + P] = const[:, C_CAUSAL:C_CAUSAL + P].T
    const[:, C_NEGQ] = _np.where((row % 32 >= 2 * DH) & (row % 32 < 3 * DH), -1.0, 0.0)
    const[:, C_NEGK] = _np.where((row % 32 >= DH) & (row % 32 < 2 * DH), -1.0, 0.0)
    const[:, C_ONEK] = _np.where((row % 32 >= R_MAX) & (row % 32 < R_MAX + 2), 1.0, 0.0)
    const[:, C_HALF:C_HALF + TT] = -0.5
    const[:, C_LESS:C_LESS + E * E] = _np.tril(_np.ones((E, E)), -1).reshape(1, E * E)
    selc = _np.zeros((2 * E, E, P), _np.float32)
    for e in range(E):
        selc[e, e, :] = 1.0
        selc[E + e, e, :] = 1.0
    selc = selc.reshape(2 * E, E * P)

    nc = _bacc.Bacc("TRN2", target_bir_lowering=False, num_devices=1)
    arrays, args = {}, []
    for name, a in [(n, inputs[n]) for n in _INS] + [("const", const), ("selc", selc)]:
        a = _np.ascontiguousarray(a)
        arrays[f"in_{name}_dram"] = a
        args.append(nc.dram_tensor(f"in_{name}_dram", a.shape, _mybir.dt.from_np(a.dtype), kind="ExternalInput").ap())
    out = nc.dram_tensor("out_0_dram", (NB, T, D), _mybir.dt.float32, kind="ExternalOutput").ap()
    resid = nc.dram_tensor("resid", (NB, T, D), _mybir.dt.float32, kind="Internal").ap()
    build(nc, *args, resid, out)
    r = _run(nc, [arrays], core_ids=[0])
    return r.results[0]["out_0_dram"]
```

```python
from contextlib import ExitStack

import concourse.bass as bass
from concourse import mybir

F32 = mybir.dt.float32
F32R = mybir.dt.float32r
BF16 = mybir.dt.bfloat16
ALU = mybir.AluOpType
ACT = mybir.ActivationFunctionType
AX_X = mybir.AxisListType.X

P = 128
D = 128
NB = 16
T = 512
TT = T // P
NT = NB * TT
H = 16
DH = D // H
LAT = 64
G = 4
NJ = H // G
NSTEP = NB * NJ
E = 8
F = 512
FC = F // P
NC = E * FC
SCALE = 1.0 / float(DH) ** 0.5
EPS_LN = 1e-5
EPS_GATE = 1e-8

C_ID = 0
C_CAUSAL = C_ID + P
C_CAUSALT = C_CAUSAL + P
C_NEGQ = C_CAUSALT + P
C_NEGK = C_NEGQ + 1
C_ONEK = C_NEGK + 1
C_HALF = C_ONEK + 1
C_MONE = C_HALF + TT
C_LESS = C_MONE + NT
C_END = C_LESS + E * E

R_MAX = 3 * DH
MX_UNITS = ((0, 0, 4), (1, 0, 2), (1, 2, 2)) + tuple((i, g, 1) for i in (2, 3) for g in range(G))
EX_UNITS = tuple((i, g, 1) for i in (0, 1) for g in range(G)) + ((2, 0, 2), (2, 2, 2), (3, 0, 4))
NU = len(MX_UNITS)
assert len(EX_UNITS) == NU
RING = 3
EX_DONE = tuple(1 + max(w for w in range(NU) if EX_UNITS[w][0] == i) for i in range(TT))


def bank_freed(w):
    before = [v - NU for v in range(NU) if v % RING == w % RING] + [v for v in range(w) if v % RING == w % RING]
    return before[-1] + 1


KEY_DMAS = 16 * G
ROW_DMAS = 16 * 2 * TT
LW2 = 2


def build(nc, x, wcd, wqu, wkvu, wcp, wg, bg, w1, b1, w2, b2, gamma, beta, const, selc, resid, out):
    with ExitStack() as ctx:
        def sb(name, shape, dt=F32, scope=ctx):
            return scope.enter_context(nc.sbuf_tensor(name, shape, dt))

        def sem(name):
            return ctx.enter_context(nc.semaphore(name))

        cst = sb("cst", [P, C_END])
        causal_b = sb("causal_b", [P, P], BF16)
        causal_t = sb("causal_t", [P, P], BF16)
        ident_b = sb("ident_b", [P, P], BF16)
        xin = sb("xin", [P, 2, T])
        xT = sb("xT", [P, NT * P])
        w1h = sb("w1h", [P, NC * P], F32R)
        w1l = sb("w1l", [P, NC * P], F32R)
        w2h = sb("w2h", [P, NC * P], F32R)
        w2l = sb("w2l", [P, NC * P], F32R)
        gam = sb("gam", [P, D])
        bet = sb("bet", [P, D])
        b1r = sb("b1r", [NC, P])
        b1T = sb("b1T", [P, NC])
        b2r = sb("b2r", [2 * E, D])
        b2h = sb("b2h", [2 * E, D], F32R)
        b2l = sb("b2l", [2 * E, D], F32R)
        bgc = sb("bgc", [E, 1])
        cwhl = sb("cwhl", [P, NT, 2 * E], F32R)
        ident = cst[:, C_ID:C_ID + P]

        scope_a = ExitStack()
        A = lambda name, shape, dt=F32: sb(name, shape, dt, scope_a)
        wcd_s = A("wcd_s", [P, LAT])
        wcdT = A("wcdT", [LAT, P])
        wup = A("wup", [LAT, D + 2 * DH])
        wcp_s = A("wcp_s", [P, D])
        wg_s = A("wg_s", [P, E])
        wgh = A("wgh", [P, E], F32R)
        wgl = A("wgl", [P, E], F32R)
        wfold = A("wfold", [P, D + 2 * DH])
        wst = A("wst", [P, NJ + 1, P])
        wsth = A("wsth", [P, NJ + 1, P], F32R)
        wstl = A("wstl", [P, NJ + 1, P], F32R)
        stats = A("stats", [P, 2, TT, 6])
        mv = A("mv", [P, 2, TT, 2])
        veps = A("veps", [P, 2, TT])
        rstd = A("rstd", [P, 2, TT])
        xn = A("xn", [P, 2, T])
        xh = A("xh", [P, 2, T], F32R)
        xl = A("xl", [P, 2, T], F32R)
        lgT = A("lgT", [E, 2, T])
        w_r = A("w_r", [P, NT, E])
        rsm = A("rsm", [P, NT])
        rss = A("rss", [P, NT])
        rank = A("rank", [P, NT, E])
        kpad = A("kpad", [P, 2, G, T], F32R)
        kh = A("kh", [P, T], F32R)
        kf = A("kf", [P, T], F32R)
        kvs = A("kvs", [P, T])
        vv = A("vv", [P, 2, TT, 32])
        qs = A("qs", [P, 4, T], F32R)
        qh = A("qh", [P, 2, T], F32R)
        pp = A("pp", [P, 2, G, T])
        pvs = A("pvs", [P, T])
        rden = A("rden", [P, TT * G])
        y = A("y", [P, 2, TT, D])
        yT = A("yT", [P, T])
        nm = A("nm", [P, G * TT])
        nmhl = A("nmhl", [P, 2, 2 * G * TT])
        nmh_r = A("nmh_r", [P, G * TT], F32R)
        ms = A("ms", [2 * G * TT, 2, P], F32R)
        wraw = A("wraw", [P, 2, F])
        cmp = xn
        scope_a.close()

        scope_b = ExitStack()
        B = lambda name, shape, dt=F32: sb(name, shape, dt, scope_b)
        zh = B("zh", [P, 2, T], F32R)
        zl = B("zl", [P, 2, T], F32R)
        selcw = B("selcw", [P, E * P])
        selr = B("selr", [P, E * P], F32R)
        cws = B("cws", [P, T], F32R)
        cwb = B("cwb", [P, 2, T])
        hf = B("hf", [P, 4, T])
        hh = B("hh", [P, 4, T], F32R)
        hl = B("hl", [P, 4, T], F32R)
        yw = B("yw", [P, 2, T])
        facc = B("facc", [P, T])
        fst = B("fst", [P, TT, 6])
        fmv = B("fmv", [P, TT, 2])
        fve = B("fve", [P, TT])
        frs = B("frs", [P, TT])
        fz = B("fz", [P, T])
        cwst = B("cwst", [P, TT * 2 * E])
        fo = B("fo", [P, 2, T])
        scope_b.close()

        ps = ctx.enter_context(nc.psum_tensor("ps", [P, 8, T], F32))
        PS_MX, PS_EX, PS_PV, PS_MISC = 0, RING, 2 * RING, 2 * RING + 1
        misc = ps[:, PS_MISC, :]

        dma_names = ("cst", "wcd", "wqu", "wkvu", "wcp", "wg", "bg", "w1", "b1", "w2", "b2", "gam", "bet", "sel")
        ld = {n: sem(f"s_ld_{n}") for n in dma_names}
        s_x = [sem(f"s_x{i}") for i in range(2)]
        s_xa = [sem(f"s_xa{i}") for i in range(2)]
        s_xr = [sem(f"s_xr{i}") for i in range(2)]
        s_xb = [sem(f"s_xb{i}") for i in range(2)]
        names = ("const_b", "wcdT_ps", "wcdT", "fold_ps", "fold", "wst0", "wst", "wsth", "wstl", "wgh", "wgl", "kz",
                 "kone", "vz", "vone", "b1_ps", "b1T", "b2h", "b2l",
                 "stat", "mv", "veps", "rstd", "xn", "xT_ps", "xT", "xh0", "xl0", "lg_ps", "lgT", "lt_ps", "lt",
                 "rt", "rexp", "rp", "cw", "wh", "wl",
                 "xh", "xl", "kv_ps", "kh", "kvs", "kf", "v_ps", "v", "q_ps", "qh", "qs", "mx_ps", "mx", "nm1",
                 "nm", "mT_ps", "mT", "ex_ps", "ex", "pv", "pvs", "pvT_ps", "rden", "y", "yT_ps", "yT",
                 "c_ps", "xo",
                 "cz", "selr", "zh", "zl", "cwst", "ct_ps", "cws", "cb_ps", "cwb", "h_ps", "hf", "hh_a", "hh_d", "hl",
                 "y_ps", "yw", "fadd", "ft_ps", "fst", "fmv", "fve", "frs", "fz", "fg", "fb", "fo", "zero")
        s = {n: sem(f"s_{n}") for n in names}
        s_passed = sem("s_passed")
        s_kpad = [sem(f"s_kpad{i}") for i in range(2)]
        s_mrow = [sem(f"s_mrow{i}") for i in range(4)]
        s_out = [sem(f"s_out{i}") for i in range(2)]

        x_v = x.rearrange("b (i p) d -> b p i d", p=P)
        out_v = out.rearrange("b (i p) d -> b p i d", p=P)
        resid_v = resid.rearrange("b (i p) d -> b p i d", p=P)

        def seq_rows(view, b):
            return view[b, :, :, :] if isinstance(b, int) else \
                view[bass.ds(b, 1), :, :, :].rearrange("a p i d -> p (a i) d")

        def stage(it, u, lag, n_all, unroll, per=1):
            assert (u - lag) % per == 0
            n = it * (unroll // per) + (u - lag) // per
            if isinstance(it, int) and not 0 <= n < n_all:
                return None
            return n

        def trips(eng, body, head=1):
            for it in range(head):
                body(it)
            with eng.Fori(head, NB // 2 - 1) as it:
                body(it)
            body(NB // 2 - 1)

        def loops(eng, body, lags, n_steps, unroll, head=1):
            total = -(-(n_steps + max(lags)) // unroll)
            full = n_steps // unroll
            for it in range(head):
                body(it)
            with eng.Fori(head, full) as it:
                body(it)
            for it in range(full, total):
                body(it)

        block = ctx.enter_context(nc.Block())

        LAG0 = dict(x=0, xT=1, lg=2, lt=3)
        LAGA = dict(kv=0, v=1, q=1, mx=2, m=3, ex=4, pv3=5, pvT=5, yT=10, c=11)
        XSLOT = {0: ("kv", 0), 1: ("v", 1), 2: ("yT", 10), 3: ("c", 11)}

        def a_idx(it, u, what):
            per = 4 if what in ("kv", "v", "yT", "c") else 1
            return stage(it, u, LAGA[what], NB if per == 4 else NSTEP, 8, per)

        def a_par(u, what):
            per = 4 if what in ("kv", "v", "yT", "c") else 1
            return (u - LAGA[what]) // per

        def plain(eng):
            eng.sem_inc(s_passed, 1)

        def pair(b, it, u, what):
            if what == "mx4":
                return b // 2 if isinstance(b, int) else it + a_par(u, "mx") // 8
            return b // 2 if isinstance(b, int) else it + a_par(u, what) // 2

        def misc_freed(it, u, slot):
            order = ("m", "q", "pvT", "x")
            at = u * 4 + order.index(slot)
            while True:
                at -= 1
                pu, ps_ = at // 4, order[at % 4]
                if isinstance(it, int) and 8 * it + pu < 0:
                    return [(s["lt"], NB)]
                what = XSLOT[pu % 4][0] if ps_ == "x" else ps_
                n = a_idx(it, pu, what)
                if n is None:
                    continue
                return {"q": [(s["qs"], n + 1)], "m": [(s["mT"], n + 1)], "pvT": [(s["y"], n + 1)],
                        "kv": [(s["kf"], n + 1), (s["kvs"], n + 1)], "v": [(s["v"], n + 1)],
                        "yT": [(s["yT"], n + 1)], "c": [(s["xo"], n + 1)]}[what]

        @block.sync
        def _(sp):
            sp.dma_start(cst[:, :], const).then_inc(ld["cst"], 16)
            sp.dma_start(wcd_s[:, :], wcd).then_inc(ld["wcd"], 16)
            sp.dma_start(wup[:, 0:D], wqu).then_inc(ld["wqu"], 16)
            sp.dma_start(wup[:, D:D + 2 * DH], wkvu).then_inc(ld["wkvu"], 16)
            sp.dma_start(wcp_s[:, :], wcp).then_inc(ld["wcp"], 16)
            sp.dma_start(wg_s[:, :], wg).then_inc(ld["wg"], 16)
            sp.dma_start(bgc[:, :], bg.rearrange("(e a) -> e a", a=1)).then_inc(ld["bg"], 16)
            sp.dma_start(b1r[:, :], b1.rearrange("e (c p) -> (e c) p", p=P)).then_inc(ld["b1"], 16)
            for r in range(2):
                sp.dma_start(b2r[r * E:(r + 1) * E, :], b2).then_inc(ld["b2"], 16)
            sp.dma_start(gam[:, :], gamma.rearrange("(a d) -> a d", a=1).to_broadcast([P, D])).then_inc(ld["gam"], 16)
            sp.dma_start(bet[:, :], beta.rearrange("(a d) -> a d", a=1).to_broadcast([P, D])).then_inc(ld["bet"], 16)

            def load_w(k):
                e = k // 2
                if k >= 2:
                    sp.wait_ge(s["wl"], k - 1)
                if k % 2 == 0:
                    sp.dma_start(wraw[:, 0, :], w1[e, :, :]).then_inc(ld["w1"], 16)
                else:
                    sp.dma_start(wraw[:, 1, :].rearrange("p (c d) -> p c d", c=FC),
                                 w2[e, :, :].rearrange("(c p) d -> p c d", p=P)).then_inc(ld["w2"], 16)

            def rows(par):
                return xin[:, par, :].rearrange("p (i d) -> p i d", i=TT)

            for par in range(2):
                sp.dma_start(rows(par), seq_rows(x_v, par)).then_inc(s_x[par], 16)
            with sp.Fori(1, NB // 2) as it:
                for par in range(2):
                    sp.wait_ge(s["xn"], it * 2 + par - 1)
                    sp.dma_start(rows(par), seq_rows(x_v, it * 2 + par)).then_inc(s_x[par], 16)
            sp.wait_ge(s["xn"], NB)

            def body(it):
                for u in range(8):
                    if isinstance(it, int) and 8 * it + u < 2 * E:
                        load_w(8 * it + u)
                    n = a_idx(it, u, "m")
                    if n is not None:
                        r4 = a_par(u, "m") % 4
                        sp.wait_ge(s["mT"], n + 1)
                        for r in range(2):
                            for i in range(TT):
                                sp.dma_start(qs[R_MAX + r:P:32, r4, bass.ts(i, P)].bitcast(F32),
                                             ms[r * G * TT + i:(r + 1) * G * TT:TT, a_par(u, "m") % 2, :].bitcast(F32))\
                                    .then_inc(s_mrow[r4], 16)
                    if u % 4 == 0:
                        b = a_idx(it, u, "kv")
                        if b is not None:
                            par = a_par(u, "kv") % 2
                            sp.wait_ge(s["kf"], b + 1)
                            if not (isinstance(b, int) and b < 2):
                                sp.wait_ge(s["ex_ps"], (4 * b - 4) * NU)
                            for g in range(G):
                                r = slice(32 * g, 32 * g + R_MAX)
                                sp.dma_start(kpad[r, par, g, :].bitcast(F32), kf[r, :].bitcast(F32))\
                                    .then_inc(s_kpad[par], 16)
                    if u % 4 == 2:
                        b = a_idx(it, u, "yT")
                        if b is not None:
                            par = a_par(u, "yT") % 2
                            if not (isinstance(b, int) and b < 2):
                                sp.wait_ge(s_xr[par], pair(b, it, u, "yT") * 16)
                            sp.dma_start(rows(par), seq_rows(x_v, b)).then_inc(s_xa[par], 16)
                    if u % 4 == 3:
                        b = a_idx(it, u, "c")
                        if b is not None:
                            par = a_par(u, "c") % 2
                            sp.wait_ge(s["xo"], b + 1)
                            sp.dma_start(seq_rows(resid_v, b), rows(par)).then_inc(s_xr[par], 16)
            loops(sp, body, LAGA.values(), NSTEP, 8, head=2)
            for par in range(2):
                sp.wait_ge(s_xr[par], 16 * (NB // 2))
            sp.wait_ge(s["xo"], NB)
            sp.wait_ge(s["cz"], 1)
            sp.dma_start(selcw[0:2 * E, :], selc).then_inc(ld["sel"], 16)

            def body_b(it):
                for par in range(2):
                    b = it * 2 + par
                    if not (isinstance(b, int) and b < 2):
                        sp.wait_ge(s["fo"], b - 1)
                    sp.dma_start(rows(par), seq_rows(resid_v, b)).then_inc(s_xb[par], 16)
                    if not (isinstance(b, int) and b == 0):
                        store(b - 1, (par + 1) % 2)

            def store(b, par):
                sp.wait_ge(s["fo"], b + 1)
                sp.dma_start(seq_rows(out_v, b), fo[:, par, :].rearrange("p (i d) -> p i d", i=TT))\
                    .then_inc(s_out[par], 16)
            trips(sp, body_b)
            store(NB - 1, 1)
            for par in range(2):
                sp.wait_ge(s_out[par], 16 * (NB // 2))

        @block.tensor
        def _(pe):
            def mm3(o, ah, al, bh, bl, start=True, stop=True, skip=False):
                pe.matmul(o, ah, bh, start=start, stop=False, skip_group_check=skip)
                pe.matmul(o, ah, bl, start=False, stop=False, skip_group_check=skip)
                return pe.matmul(o, al, bh, start=False, stop=stop, skip_group_check=skip)

            pe.wait_ge(ld["cst"], 16)
            pe.wait_ge(ld["wcd"], 16)
            pe.transpose(ps[0:LAT, 0, 0:P], wcd_s[:, :], ident).then_inc(s["wcdT_ps"], 1)
            pe.wait_ge(s["wcdT"], 1)
            pe.wait_ge(ld["wqu"], 16)
            pe.wait_ge(ld["wkvu"], 16)
            pe.matmul(ps[:, 1, 0:D + 2 * DH], wcdT[:, :], wup[:, :], start=True, stop=True).then_inc(s["fold_ps"], 1)
            pe.wait_ge(ld["b1"], 16)
            pe.transpose(ps[:, 2, 0:NC], b1r[:, :], ident[0:NC, 0:NC]).then_inc(s["b1_ps"], 1)
            pe.wait_ge(s["wgl"], 1)

            def body0(it):
                for u in range(2):
                    b = stage(it, u, LAG0["xT"], NB, 2)
                    if b is not None:
                        pe.wait_ge(s["xn"], b + 1)
                        if not (isinstance(it, int) and it == 0 and u == 1):
                            pe.wait_ge(s["xl0"], b)
                        for i in range(TT):
                            t = pe.transpose(ps[:, 3, bass.ts(i, P)], xn[:, (u - 1) % 2, bass.ts(i, P)], ident)
                        t.then_inc(s["xT_ps"], 1)
                    b = stage(it, u, LAG0["lg"], NB, 2)
                    if b is not None:
                        par = (u - 2) % 2
                        pe.wait_ge(s["xl0"], b + 1)
                        if not (isinstance(it, int) and 2 * it + u == 2):
                            pe.wait_ge(s["lgT"], b)
                        mm3(ps[0:E, 4, :], wgh[:, :], wgl[:, :], xh[:, par, :], xl[:, par, :]).then_inc(s["lg_ps"], 1)
                    b = stage(it, u, LAG0["lt"], NB, 2)
                    if b is not None:
                        pe.wait_ge(s["lgT"], b + 1)
                        if not (isinstance(it, int) and 2 * it + u == 3):
                            pe.wait_ge(s["lt"], b)
                        for i in range(TT):
                            t = pe.matmul(misc[:, i * E:(i + 1) * E], lgT[:, (u - 3) % 2, bass.ts(i, P)],
                                          cst[0:E, C_ID:C_ID + E], start=True, stop=True)
                        t.then_inc(s["lt_ps"], 1)
            loops(pe, body0, LAG0.values(), NB, 2, head=2)

            pe.wait_ge(s["wstl"], 1)
            pe.wait_ge(s["const_b"], 2)
            pe.wait_ge(s["kone"], 1)
            pe.wait_ge(s["vone"], 1)
            pe.wait_ge(s["b1T"], 1)

            def misc_wait(it, u, slot):
                for sm, v in misc_freed(it, u, slot):
                    pe.wait_ge(sm, v)

            def body(it):
                for u in range(8):
                    n_mx, n_ex = a_idx(it, u, "mx"), a_idx(it, u, "ex")
                    first = isinstance(it, int) and it == 0

                    def units(w):
                        masks = []
                        if n_mx is not None:
                            i, g0, gn = MX_UNITS[w]
                            cols = (i + 1) * P
                            r4, kb = a_par(u, "mx") % 4, (a_par(u, "mx") // 4) % 2
                            if w == 0:
                                pe.wait_ge(s["qs"], n_mx + 1)
                                if a_par(u, "mx") % 4 == 0:
                                    b = n_mx // 4 if isinstance(n_mx, int) else it * 2 + a_par(u, "mx") // 4
                                    pe.wait_ge(s_kpad[kb], (pair(b, it, u, "mx4") + 1) * KEY_DMAS)
                            if not (first and n_mx == 0 and w < RING):
                                pe.wait_ge(s["mx"], n_mx * NU + bank_freed(w))
                            o = ps[:, PS_MX + w % RING, :]
                            for h in range(gn):
                                pe.matmul(o[:, h * cols:(h + 1) * cols], qs[:, r4, bass.ts(i, P)],
                                          kpad[:, kb, g0 + h, 0:cols], start=(h == 0), stop=False,
                                          skip_group_check=True)
                                masks.append((o[:, h * cols + i * P:(h + 1) * cols], causal_b, h == gn - 1, "mx_ps"))
                        if n_ex is not None:
                            i, g0, gn = EX_UNITS[w]
                            cols = T - i * P
                            r4, kb = a_par(u, "ex") % 4, (a_par(u, "ex") // 4) % 2
                            if w == 0:
                                pe.wait_ge(s_mrow[r4], (n_ex // 4 + 1) * ROW_DMAS if isinstance(n_ex, int) else
                                           (it * 2 + a_par(u, "ex") // 4 + 1) * ROW_DMAS)
                            if not (first and n_ex == 0 and w < RING):
                                pe.wait_ge(s["ex"], n_ex * NU + bank_freed(w))
                            o = ps[:, PS_EX + w % RING, :]
                            for h in range(gn):
                                pe.matmul(o[:, h * cols:(h + 1) * cols], kpad[:, kb, g0 + h, bass.ts(i, P)],
                                          qs[:, r4, i * P:T], start=(h == 0), stop=False, skip_group_check=True)
                                masks.append((o[:, h * cols:h * cols + P], causal_t, h == gn - 1, "ex_ps"))
                        for o, mask, last, done in masks:
                            mm = pe.matmul(o, ident_b[:, :], mask[:, :], start=False, stop=last,
                                           skip_group_check=True)
                            if last:
                                mm.then_inc(s[done], 1)

                    def pv(i, what="ex"):
                        n = a_idx(it, u, what)
                        if n is None:
                            return
                        vb = (a_par(u, what) // 4) % 2
                        if i == 0 and not (isinstance(n, int) and n == 0):
                            pe.wait_ge(s["pvs"], n)
                        pe.wait_ge(s["ex"], n * NU + EX_DONE[i])
                        for g in range(G):
                            mm = pe.matmul(ps[32 * g:32 * g + 32, PS_PV, i * P:T], vv[:, vb, i, :],
                                           pp[:, i % 2, g, 0:T - i * P], start=(i == 0), stop=(i == TT - 1))
                        mm.then_inc(s["pv"], 1)

                    def q_proj():
                        n = a_idx(it, u, "q")
                        if n is None:
                            return
                        misc_wait(it, u, "q")
                        j, kb = a_par(u, "q") % 4, (a_par(u, "q") // 4) % 2
                        mm3(misc, wsth[:, j, :], wstl[:, j, :], xh[:, kb, :], xl[:, kb, :]).then_inc(s["q_ps"], 1)

                    def max_rows():
                        n = a_idx(it, u, "m")
                        if n is None:
                            return
                        misc_wait(it, u, "m")
                        pe.wait_ge(s["nm"], n + 1)
                        pe.transpose(misc[0:2 * G * TT, 0:P], nmhl[:, a_par(u, "m") % 2, :], ident)\
                            .then_inc(s["mT_ps"], 1)

                    def pv_turn():
                        n = a_idx(it, u, "pvT")
                        if n is None:
                            return
                        misc_wait(it, u, "pvT")
                        pe.wait_ge(s["pvs"], n + 1)
                        for i in range(TT):
                            t = pe.transpose(misc[:, bass.ts(i, P)], pvs[:, bass.ts(i, P)], ident)
                        t.then_inc(s["pvT_ps"], 1)

                    def extra():
                        what, _ = XSLOT[u % 4]
                        n = a_idx(it, u, what)
                        if n is None:
                            return
                        misc_wait(it, u, "x")
                        par = a_par(u, what) % 2
                        if what == "kv":
                            pe.wait_ge(s["xl"], n + 1)
                            mm3(misc, wsth[:, NJ, :], wstl[:, NJ, :], xh[:, par, :], xl[:, par, :])\
                                .then_inc(s["kv_ps"], 1)
                        elif what == "v":
                            pe.wait_ge(s["kvs"], n + 1)
                            for i in range(TT):
                                t = pe.transpose(misc[:, bass.ts(i, P)], kvs[:, bass.ts(i, P)], ident)
                            t.then_inc(s["v_ps"], 1)
                        elif what == "yT":
                            for i in range(TT):
                                t = pe.transpose(misc[:, bass.ts(i, P)], y[:, par, i, :], ident)
                            t.then_inc(s["yT_ps"], 1)
                        else:
                            pe.wait_ge(s["yT"], n + 1)
                            for i in range(TT):
                                t = pe.matmul(misc[:, bass.ts(i, P)], yT[:, bass.ts(i, P)], wcp_s[:, :],
                                              start=True, stop=True)
                            t.then_inc(s["c_ps"], 1)

                    units(0)
                    pv(3, "pv3")
                    units(1)
                    max_rows()
                    units(2)
                    units(3)
                    q_proj()
                    units(4)
                    units(5)
                    pv(0)
                    units(6)
                    pv_turn()
                    units(7)
                    units(8)
                    pv(1)
                    extra()
                    units(9)
                    units(10)
                    pv(2)
            loops(pe, body, LAGA.values(), NSTEP, 8)

            pe.wait_ge(s["selr"], 1)
            pe.wait_ge(s["wl"], 2 * E)
            pe.wait_ge(s["b2l"], 1)

            def turn_out(b):
                pe.wait_ge(s["fadd"], (b + 1) * (E - 1))
                if not (isinstance(b, int) and b == 0):
                    pe.wait_ge(s["fz"], b)
                for i in range(TT):
                    o = misc[:, bass.ts(i, P)]
                    pe.matmul(o, cws[0:2 * E, bass.ts(i, P)], b2h[:, :], start=True, stop=False)
                    pe.matmul(o, cws[0:2 * E, bass.ts(i, P)], b2l[:, :], start=False, stop=False)
                    t = pe.matmul(o, facc[:, bass.ts(i, P)], ident, start=False, stop=True)
                t.then_inc(s["ft_ps"], 1)

            def body_b(it):
                for par in range(2):
                    b = it * 2 + par
                    first = isinstance(b, int) and b == 0
                    for c in range(NC + LW2):
                        if c < NC:
                            if c == 0:
                                pe.wait_ge(s["zl"], b + 1)
                            if not (first and c < 4):
                                pe.wait_ge(s["hf"], b * NC + c - 3)
                            mm3(ps[:, c % 4, :], w1h[:, bass.ts(c, P)], w1l[:, bass.ts(c, P)],
                                zh[:, par, :], zl[:, par, :]).then_inc(s["h_ps"], 1)
                        if c == 2:
                            if not first:
                                turn_out(b - 1)
                            pe.wait_ge(s["cwst"], b + 1)
                            if not first:
                                pe.wait_ge(s["cwb"], b * E)
                            for i in range(TT):
                                t = pe.transpose(ps[0:2 * E, 6, bass.ts(i, P)], cwst[:, bass.ts(i, 2 * E)], ident)
                            t.then_inc(s["ct_ps"], 1)
                        e = c // FC - 1
                        if c >= FC and c % FC == 0:
                            if e == 0:
                                pe.wait_ge(s["cws"], b + 1)
                            else:
                                pe.wait_ge(s["cwb"], b * E + e)
                            pe.matmul(ps[:, 6, :], selr[:, bass.ts(e, P)], cws[:, :], start=True, stop=True)\
                                .then_inc(s["cb_ps"], 1)
                        if c >= LW2:
                            c2 = c - LW2
                            e2, k = c2 // FC, c2 % FC
                            if k == 0 and not (first and e2 < 2):
                                pe.wait_ge(s["yw"], b * E + e2 - 1)
                            pe.wait_ge(s["hl"], b * NC + c2 + 1)
                            mm = mm3(ps[:, 4 + e2 % 2, :], w2h[:, bass.ts(c2, P)], w2l[:, bass.ts(c2, P)],
                                     hh[:, c2 % 4, :], hl[:, c2 % 4, :], start=(k == 0), stop=(k == FC - 1))
                            mm.then_inc(s["y_ps"], 1)
            trips(pe, body_b)
            turn_out(NB - 1)

        @block.scalar
        def _(act):
            def copy(o, i):
                return act.activation(o, i, ACT.Copy)

            act.wait_ge(ld["cst"], 16)
            copy(causal_b[:, :], cst[:, C_CAUSAL:C_CAUSAL + P])
            copy(causal_t[:, :], cst[:, C_CAUSALT:C_CAUSALT + P]).then_inc(s["const_b"], 1)
            copy(ident_b[:, :], ident).then_inc(s["const_b"], 1)
            act.wait_ge(s["wcdT_ps"], 1)
            copy(wcdT[:, :], ps[0:LAT, 0, 0:P]).then_inc(s["wcdT"], 1)
            act.wait_ge(s["fold_ps"], 1)
            copy(wfold[:, :], ps[:, 1, 0:D + 2 * DH]).then_inc(s["fold"], 1)
            act.wait_ge(s["b1_ps"], 1)
            copy(b1T[:, :], ps[:, 2, 0:NC]).then_inc(s["b1T"], 1)
            act.wait_ge(ld["wg"], 16)
            copy(wgh[:, :], wg_s[:, :]).then_inc(s["wgh"], 1)
            act.wait_ge(ld["b2"], 32)
            copy(b2h[:, :], b2r[:, :]).then_inc(s["b2h"], 1)
            act.wait_ge(s["wst"], 1)
            copy(wsth[:, :, :], wst[:, :, :]).then_inc(s["wsth"], 1)
            act.wait_ge(ld["bg"], 16)

            def body0(it):
                for u in range(2):
                    b = stage(it, u, LAG0["xT"], NB, 2)
                    if b is not None:
                        par = (u - 1) % 2
                        act.wait_ge(s["xT_ps"], b + 1)
                        if not (isinstance(it, int) and 2 * it + u < 3):
                            act.wait_ge(s["lg_ps"], b - 1)
                        copy(xh[:, par, :], ps[:, 3, :]).then_inc(s["xh0"], 1)
                        copy(xT[:, bass.ts(b, T)], ps[:, 3, :]).then_inc(s["xT"], 1)
                    b = stage(it, u, LAG0["lg"], NB, 2)
                    if b is not None:
                        par = (u - 2) % 2
                        act.wait_ge(s["lg_ps"], b + 1)
                        if not (isinstance(it, int) and 2 * it + u < 4):
                            act.wait_ge(s["lt_ps"], b - 1)
                        act.activation(lgT[:, par, :], ps[0:E, 4, :], ACT.Identity, bias=bgc[:, :])\
                            .then_inc(s["lgT"], 1)
            loops(act, body0, LAG0.values(), NB, 2, head=2)
            act.wait_ge(s["rt"], 2)
            act.activation(w_r[:, :, :], w_r[:, :, :], ACT.Exp).then_inc(s["rexp"], 1)

            def body(it):
                for u in range(8):
                    n_ex = a_idx(it, u, "ex")
                    if u % 4 == 0:
                        b = a_idx(it, u, "kv")
                        if b is not None:
                            if not (isinstance(b, int) and b < 2):
                                act.wait_ge(s["q_ps"], 4 * b - 4)
                            else:
                                act.wait_ge(s["lg_ps"], NB)
                            act.wait_ge(s["xT"], NB)
                            copy(xh[:, a_par(u, "kv") % 2, :], xT[:, bass.ts(b, T)]).then_inc(s["xh"], 1)

                    def exp_unit(w):
                        if n_ex is None:
                            return
                        i, g0, gn = EX_UNITS[w]
                        cols = T - i * P
                        act.wait_ge(s["ex_ps"], n_ex * NU + w + 1)
                        if g0 == 0 and not (isinstance(n_ex, int) and n_ex == 0 and i < 2):
                            act.wait_ge(s["pv"], n_ex * TT + i - 1)
                        act.activation(pp[:, i % 2, g0:g0 + gn, 0:cols],
                                       ps[:, PS_EX + w % RING, 0:gn * cols].rearrange("p (g c) -> p g c", g=gn),
                                       ACT.Exp, scale=SCALE).then_inc(s["ex"], 1)

                    exp_unit(0)
                    n = a_idx(it, u, "pvT")
                    if n is not None:
                        act.wait_ge(s["pv"], (n + 1) * TT)
                        if not (isinstance(n, int) and n == 0):
                            act.wait_ge(s["pvT_ps"], n)
                        copy(pvs[:, :], ps[:, PS_PV, :]).then_inc(s["pvs"], 1)
                    exp_unit(1)
                    n = a_idx(it, u, "m")
                    if n is not None:
                        act.wait_ge(s["mT_ps"], n + 1)
                        if not (isinstance(n, int) and n < 2):
                            r4 = (a_par(u, "m") - 2) % 4
                            act.wait_ge(s_mrow[r4], ((n - 2) // 4 + 1) * ROW_DMAS if isinstance(n, int) else
                                        (it * 2 + (a_par(u, "m") - 2) // 4 + 1) * ROW_DMAS)
                        copy(ms[:, a_par(u, "m") % 2, :], misc[0:2 * G * TT, 0:P]).then_inc(s["mT"], 1)
                    exp_unit(2)
                    exp_unit(3)
                    n = a_idx(it, u, "q")
                    if n is not None:
                        act.wait_ge(s["q_ps"], n + 1)
                        if not (isinstance(n, int) and n < 2):
                            act.wait_ge(s["qs"], n - 1)
                        copy(qh[:, a_par(u, "q") % 2, :], misc).then_inc(s["qh"], 1)
                    for w in range(4, 9):
                        exp_unit(w)
                    what, _ = XSLOT[u % 4]
                    n = a_idx(it, u, what)
                    if n is not None:
                        par = a_par(u, what) % 2
                        if what == "kv":
                            act.wait_ge(s["kv_ps"], n + 1)
                            if not (isinstance(n, int) and n == 0):
                                act.wait_ge(s["kf"], n)
                                act.wait_ge(s["v_ps"], n)
                            copy(kh[:, :], misc).then_inc(s["kh"], 1)
                            copy(kvs[:, :], misc).then_inc(s["kvs"], 1)
                        elif what == "v":
                            act.wait_ge(s["v_ps"], n + 1)
                            if not (isinstance(n, int) and n < 2):
                                act.wait_ge(s["pv"], (4 * n - 4) * TT)
                            copy(vv[:, par, :, 0:DH], misc.rearrange("p (i c) -> p i c", i=TT)
                                 [:, :, R_MAX:R_MAX + DH]).then_inc(s["v"], 1)
                        elif what == "yT":
                            act.wait_ge(s["yT_ps"], n + 1)
                            if not (isinstance(n, int) and n == 0):
                                act.wait_ge(s["c_ps"], n)
                            copy(yT[:, :], misc).then_inc(s["yT"], 1)
                    for w in range(9, NU):
                        exp_unit(w)
            loops(act, body, LAGA.values(), NSTEP, 8, head=2)

            act.wait_ge(s["xo"], NB)
            act.wait_ge(ld["sel"], 16)
            copy(selr[:, :], selcw[:, :]).then_inc(s["selr"], 1)

            def split_x(b, par, first):
                if not first:
                    act.wait_ge(s["h_ps"], (b - 1) * NC)
                copy(zh[:, par, :], xT[:, bass.ts(b, T)]).then_inc(s["zh"], 1)
            split_x(0, 0, True)

            def body_b(it):
                for par in range(2):
                    b = it * 2 + par
                    first = isinstance(b, int) and b == 0
                    if first:
                        act.wait_ge(s["cw"], 1)
                    else:
                        act.wait_ge(s["ct_ps"], b)
                    copy(cwst[:, :], cwhl[:, bass.ts(b, TT), :].bitcast(F32).rearrange("p i r -> p (i r)"))\
                        .then_inc(s["cwst"], 1)
                    for c in range(NC):
                        act.wait_ge(s["h_ps"], b * NC + c + 1)
                        if not (first and c < 4):
                            act.wait_ge(s["hl"], b * NC + c - 3)
                        act.activation(hf[:, c % 4, :], ps[:, c % 4, :], ACT.Gelu, bias=b1T[:, c:c + 1])\
                            .then_inc(s["hf"], 1)
                        if c % 2:
                            act.wait_ge(s["hf"], b * NC + c + 1)
                            if not (first and c < 4):
                                act.wait_ge(s["y_ps"], b * NC + c - 3)
                            copy(hh[:, c % 4, :], hf[:, c % 4, :]).then_inc(s["hh_a"], 1)
                        if c == 2:
                            act.wait_ge(s["ct_ps"], b + 1)
                            if not first:
                                act.wait_ge(s["ft_ps"], b)
                            else:
                                act.wait_ge(s["cz"], 2)
                            copy(cws[0:2 * E, :], ps[0:2 * E, 6, :]).then_inc(s["cws"], 1)
                        e = c // FC - 1
                        if c >= FC and c % FC == 0 or c == NC - 1:
                            if c == NC - 1:
                                e = E - 1
                            act.wait_ge(s["cb_ps"], b * E + e + 1)
                            if not (first and e < 2):
                                act.wait_ge(s["yw"], b * E + e - 1)
                            copy(cwb[:, e % 2, :], ps[:, 6, :]).then_inc(s["cwb"], 1)
                        if c == NC // 2 and not (isinstance(b, int) and b == NB - 1):
                            split_x(b + 1, (par + 1) % 2, first)
            trips(act, body_b)

        @block.vector
        def _(dve):
            negq = cst[:, C_NEGQ:C_NEGQ + 1]
            negk = cst[:, C_NEGK:C_NEGK + 1]
            dve.memset(kpad[:, :, :, :].rearrange("p a g t -> p (a g t)").bitcast(F32), 0.0).then_inc(s["kz"], 1)
            dve.memset(wst[:, :, :], 0.0).then_inc(s["wst0"], 1)
            dve.wait_ge(ld["cst"], 16)
            dve.wait_ge(s["kz"], 1)
            for par in range(2):
                for g in range(G):
                    o = kpad[32 * g:32 * g + 32, par, g, :]
                    t = dve.tensor_scalar(o, o.bitcast(F32), cst[32 * g:32 * g + 32, C_ONEK:C_ONEK + 1], None, ALU.add)
            t.then_inc(s["kone"], 1)
            dve.wait_ge(s["fold"], 1)
            dve.wait_ge(s["wst0"], 1)
            for r in range(3):
                dve.tensor_copy(wst[:, 0:NJ, :].rearrange("p j (g c) -> p (j g) c", g=G)[:, :, r * DH:(r + 1) * DH],
                                wfold[:, 0:D].rearrange("p (h c) -> p h c", h=H))
                for g in range(G):
                    dve.tensor_copy(wst[:, NJ, 32 * g + r * DH:32 * g + (r + 1) * DH], wfold[:, D:D + DH])
            for g in range(G):
                t = dve.tensor_copy(wst[:, NJ, 32 * g + R_MAX:32 * g + R_MAX + DH], wfold[:, D + DH:D + 2 * DH])
            t.then_inc(s["wst"], 1)
            dve.wait_ge(s["wgh"], 1)
            dve.tensor_tensor(wgl[:, :], wg_s[:, :], wgh[:, :].bitcast(F32), ALU.subtract).then_inc(s["wgl"], 1)
            dve.wait_ge(s["b2h"], 1)
            dve.tensor_tensor(b2l[:, :], b2r[:, :], b2h[:, :].bitcast(F32), ALU.subtract).then_inc(s["b2l"], 1)
            dve.wait_ge(s["wsth"], 1)
            dve.wait_ge(s["wst"], 1)
            dve.tensor_tensor(wstl[:, :, :], wst[:, :, :], wsth[:, :, :].bitcast(F32), ALU.subtract)\
                .then_inc(s["wstl"], 1)

            def body0(it):
                for u in range(2):
                    b = stage(it, u, LAG0["x"], NB, 2)
                    if b is not None:
                        dve.wait_ge(s_x[u], (it + 1) * 16)
                        if not (isinstance(it, int) and it == 0):
                            dve.wait_ge(s["xn"], b - 1)
                        for i in range(TT):
                            t = dve.bn_stats(stats[:, u, i, :], xin[:, u, bass.ts(i, D)])
                        t.then_inc(s["stat"], 1)
                        dve.wait_ge(s["stat"], b + 1)
                        plain(dve)
                        for i in range(TT):
                            t = dve.bn_aggr(mv[:, u, i, :], stats[:, u, i, :])
                        t.then_inc(s["mv"], 1)
                    b = stage(it, u, LAG0["xT"], NB, 2)
                    if b is not None:
                        par = (u - 1) % 2
                        dve.wait_ge(s["rstd"], b + 1)
                        dve.wait_ge(s["mv"], b + 1)
                        if not (isinstance(it, int) and 2 * it + u < 3):
                            dve.wait_ge(s["xT_ps"], b - 1)
                        for i in range(TT):
                            t = dve.tensor_scalar(xn[:, par, bass.ts(i, D)], xin[:, par, bass.ts(i, D)],
                                                  mv[:, par, i, 0:1], rstd[:, par, i:i + 1], ALU.subtract, ALU.mult)
                        t.then_inc(s["xn"], 1)
                        dve.wait_ge(s["xT"], b + 1)
                        dve.wait_ge(s["xh0"], b + 1)
                        if not (isinstance(it, int) and 2 * it + u < 3):
                            dve.wait_ge(s["lg_ps"], b - 1)
                        dve.tensor_tensor(xl[:, par, :], ps[:, 3, :], xh[:, par, :].bitcast(F32), ALU.subtract)\
                            .then_inc(s["xl0"], 1)
                    b = stage(it, u, LAG0["lt"], NB, 2)
                    if b is not None:
                        dve.wait_ge(s["lt_ps"], b + 1)
                        dve.tensor_copy(w_r[:, bass.ts(b, TT), :], misc[:, 0:TT * E].rearrange("p (i e) -> p i e", i=TT))\
                            .then_inc(s["lt"], 1)
            loops(dve, body0, LAG0.values(), NB, 2, head=2)

            wide = lambda a: a.rearrange("p (t a) -> p t a", a=1).to_broadcast([P, NT, E])
            dve.wait_ge(s["lt"], NB)
            dve.tensor_reduce(rsm[:, :], w_r[:, :, :], AX_X, ALU.max).then_inc(s["rt"], 1)
            dve.wait_ge(s["rt"], 1)
            dve.tensor_tensor(w_r[:, :, :], w_r[:, :, :], wide(rsm[:, :]), ALU.subtract).then_inc(s["rt"], 1)

            def body(it):
                for u in range(8):
                    n_mx = a_idx(it, u, "mx")
                    if u % 4 == 0:
                        b = a_idx(it, u, "kv")
                        if b is not None:
                            dve.wait_ge(s["xh"], b + 1)
                            par = a_par(u, "kv") % 2
                            dve.tensor_tensor(xl[:, par, :], xT[:, bass.ts(b, T)], xh[:, par, :].bitcast(F32),
                                              ALU.subtract).then_inc(s["xl"], 1)

                    def reduce(w):
                        if n_mx is None:
                            return
                        i, g0, gn = MX_UNITS[w]
                        cols = (i + 1) * P
                        dve.wait_ge(s["mx_ps"], n_mx * NU + w + 1)
                        if w == 0 and not (isinstance(n_mx, int) and n_mx == 0):
                            dve.wait_ge(s["nm"], n_mx)
                        dve.tensor_reduce(nm[:, :].rearrange("p (g i) -> p g i", g=G)[:, g0:g0 + gn, i],
                                          ps[:, PS_MX + w % RING, 0:gn * cols].rearrange("p (g c) -> p g c", g=gn),
                                          AX_X, ALU.max, negate=True).then_inc(s["mx"], 1)

                    for w in range(4):
                        reduce(w)
                    n = a_idx(it, u, "q")
                    if n is not None:
                        par = a_par(u, "q")
                        dve.wait_ge(s["qh"], n + 1)
                        if not (isinstance(n, int) and n < 4):
                            dve.wait_ge(s["ex_ps"], (n - 3) * NU)
                        dve.scalar_tensor_tensor(out=qs[:, par % 4, :], in0=qh[:, par % 2, :].bitcast(F32), scalar=negq,
                                                 in1=misc, op0=ALU.mult, op1=ALU.add).then_inc(s["qs"], 1)
                    for w in range(4, 7):
                        reduce(w)
                    n = a_idx(it, u, "pvT")
                    if n is not None:
                        par = a_par(u, "pvT")
                        dve.wait_ge(s["pvT_ps"], n + 1)
                        sums = misc.rearrange("p (n c) -> p n c", c=32)
                        dve.reciprocal(rden[:, :].rearrange("p (n a) -> p n a", a=1), sums[:, :, DH:DH + 1])\
                            .then_inc(s["rden"], 1)
                        dve.wait_ge(s["rden"], n + 1)
                        if par % 4 == 0 and not (isinstance(n, int) and n < 8):
                            dve.wait_ge(s["yT_ps"], (n if isinstance(n, int) else 0) // 4 - 1 if isinstance(n, int)
                                        else it * 2 + par // 4 - 1)
                        j = par % 4
                        dve.tensor_tensor(
                            y[:, (par // 4) % 2, :, j * G * DH:(j + 1) * G * DH].rearrange("p i (g c) -> p i g c", g=G),
                            misc.rearrange("p (i g c) -> p i g c", i=TT, g=G)[:, :, :, 0:DH],
                            rden[:, :].rearrange("p (i g a) -> p i g a", i=TT, a=1).to_broadcast([P, TT, G, DH]),
                            ALU.mult).then_inc(s["y"], 1)
                    reduce(7)
                    reduce(8)
                    what, _ = XSLOT[u % 4]
                    n = a_idx(it, u, what)
                    if n is not None and what == "kv":
                        dve.wait_ge(s["kh"], n + 1)
                        dve.wait_ge(s["kvs"], n + 1)
                        if not (isinstance(n, int) and n == 0):
                            dve.wait_ge(s_kpad[(a_par(u, what) - 1) % 2], (n - 1) // 2 * KEY_DMAS + KEY_DMAS
                                        if isinstance(n, int) else (it + (a_par(u, what) - 1) // 2 + 1) * KEY_DMAS)
                        dve.scalar_tensor_tensor(out=kf[:, :], in0=kh[:, :].bitcast(F32), scalar=negk, in1=misc,
                                                 op0=ALU.mult, op1=ALU.add).then_inc(s["kf"], 1)
                    if n is not None and what == "c":
                        dve.wait_ge(s["c_ps"], n + 1)
                        par = a_par(u, what) % 2
                        dve.wait_ge(s_xa[par], (pair(n, it, u, what) + 1) * 16)
                        xb = xin[:, par, :]
                        dve.tensor_tensor(xb, xb, misc, ALU.add).then_inc(s["xo"], 1)
                    for w in range(9, NU):
                        reduce(w)
                    if n_mx is not None:
                        par = a_par(u, "mx") % 2
                        dve.wait_ge(s["mx"], (n_mx + 1) * NU)
                        dve.tensor_copy(nmh_r[:, :], nm[:, :]).then_inc(s["nm1"], 1)
                        dve.wait_ge(s["nm1"], n_mx + 1)
                        if not (isinstance(n_mx, int) and n_mx < 2):
                            dve.wait_ge(s["mT_ps"], n_mx - 1)
                        dve.tensor_copy(nmhl[:, par, 0:G * TT], nmh_r[:, :].bitcast(F32))
                        dve.tensor_tensor(nmhl[:, par, G * TT:], nm[:, :], nmh_r[:, :].bitcast(F32), ALU.subtract)\
                            .then_inc(s["nm"], 1)
            loops(dve, body, LAGA.values(), NSTEP, 8, head=2)

            dve.wait_ge(s["c_ps"], NB)
            dve.wait_ge(s["xo"], NB)
            dve.wait_ge(s["cw"], 1)
            dve.memset(selcw[:, :], 0.0).then_inc(s["cz"], 1)
            dve.memset(cws[:, :].bitcast(F32), 0.0).then_inc(s["cz"], 1)

            def split_x(b, par):
                dve.wait_ge(s["zh"], b + 1)
                dve.tensor_tensor(zl[:, par, :], xT[:, bass.ts(b, T)], zh[:, par, :].bitcast(F32), ALU.subtract)\
                    .then_inc(s["zl"], 1)
            split_x(0, 0)

            def weigh(b, e, first):
                dve.wait_ge(s["y_ps"], b * NC + (e + 1) * FC)
                dve.wait_ge(s["cwb"], b * E + e + 1)
                if e == 0:
                    if not first:
                        dve.wait_ge(s["ft_ps"], b)
                    o = facc[:, :]
                else:
                    if not (first and e < 3):
                        dve.wait_ge(s["fadd"], b * (E - 1) + max(e - 2, 0))
                    o = yw[:, e % 2, :]
                dve.tensor_tensor(o, ps[:, 4 + e % 2, :], cwb[:, e % 2, :], ALU.mult).then_inc(s["yw"], 1)

            def out_stats(b):
                dve.wait_ge(s["ft_ps"], b + 1)
                if not (isinstance(b, int) and b == 0):
                    dve.wait_ge(s["fz"], b)
                for i in range(TT):
                    t = dve.bn_stats(fst[:, i, :], misc[:, bass.ts(i, D)])
                t.then_inc(s["fst"], 1)
                dve.wait_ge(s["fst"], b + 1)
                plain(dve)
                for i in range(TT):
                    t = dve.bn_aggr(fmv[:, i, :], fst[:, i, :])
                t.then_inc(s["fmv"], 1)

            def out_norm(b):
                dve.wait_ge(s["frs"], b + 1)
                dve.wait_ge(s["fmv"], b + 1)
                if not (isinstance(b, int) and b == 0):
                    dve.wait_ge(s["fo"], b)
                for i in range(TT):
                    t = dve.tensor_scalar(fz[:, bass.ts(i, D)], misc[:, bass.ts(i, D)], fmv[:, i, 0:1],
                                          frs[:, i:i + 1], ALU.subtract, ALU.mult)
                t.then_inc(s["fz"], 1)

            def body_b(it):
                for par in range(2):
                    b = it * 2 + par
                    first = isinstance(b, int) and b == 0
                    for c in range(NC):
                        dve.wait_ge(s["hf"], b * NC + c + 1)
                        if not (first and c < 4):
                            dve.wait_ge(s["y_ps"], b * NC + c - 3)
                        if c % 2 == 0:
                            dve.tensor_copy(hh[:, c % 4, :], hf[:, c % 4, :]).then_inc(s["hh_d"], 1)
                            dve.wait_ge(s["hh_d"], b * (NC // 2) + c // 2 + 1)
                        else:
                            dve.wait_ge(s["hh_a"], b * (NC // 2) + c // 2 + 1)
                        dve.tensor_tensor(hl[:, c % 4, :], hf[:, c % 4, :], hh[:, c % 4, :].bitcast(F32), ALU.subtract)\
                            .then_inc(s["hl"], 1)
                        if c % FC == 1 and c > FC:
                            weigh(b, (c - 5) // FC, first)
                        if c == 3 and not first:
                            out_stats(b - 1)
                        if c == 6 and not first:
                            out_norm(b - 1)
                        if c == NC // 2 + 2 and not (isinstance(b, int) and b == NB - 1):
                            split_x(b + 1, (par + 1) % 2)
                    weigh(b, E - 1, first)
            trips(dve, body_b)
            out_stats(NB - 1)
            out_norm(NB - 1)

        @block.gpsimd
        def _(pool):
            half = cst[:, C_HALF:C_HALF + TT]
            pool.memset(vv[:, :, :, :], 0.0).then_inc(s["vz"], 1)
            pool.wait_ge(s["vz"], 1)
            pool.memset(vv[:, :, :, DH:DH + 1], 1.0).then_inc(s["vone"], 1)
            pool.wait_ge(ld["cst"], 16)

            def body0(it):
                for u in range(2):
                    b = stage(it, u, LAG0["x"], NB, 2)
                    if b is None:
                        continue
                    pool.wait_ge(s["mv"], b + 1)
                    if not (isinstance(it, int) and it == 0):
                        pool.wait_ge(s["xn"], b - 1)
                    plain(pool)
                    pool.tensor_scalar(veps[:, u, :], mv[:, u, :, 1], EPS_LN, None, ALU.add).then_inc(s["veps"], 1)
                    pool.wait_ge(s["veps"], b + 1)
                    pool.tensor_tensor(rstd[:, u, :], veps[:, u, :], half, ALU.pow).then_inc(s["rstd"], 1)
            body0(0)
            with pool.Fori(1, NB // 2) as it:
                body0(it)


            def router():
                count = [0]

                def then(ins):
                    count[0] += 1
                    ins.then_inc(s["rp"], 1)
                    pool.wait_ge(s["rp"], count[0])

                def sum8(o, a, n):
                    then(pool.tensor_tensor(a[:, 0:n, 0:4], a[:, 0:n, 0:4], a[:, 0:n, 4:8], ALU.add))
                    then(pool.tensor_tensor(a[:, 0:n, 0:2], a[:, 0:n, 0:2], a[:, 0:n, 2:4], ALU.add))
                    then(pool.tensor_tensor(o, a[:, 0:n, 0], a[:, 0:n, 1], ALU.add))

                pool.wait_ge(s["rexp"], 1)
                ca = cmp[:, 0, :].rearrange("p (n f) -> p n f", f=E)
                cb = cmp[:, 1, :].rearrange("p (n f) -> p n f", f=E)
                then(pool.tensor_copy(ca, w_r[:, :, :]))
                sum8(rss[:, :], ca, NT)
                NG = T // (E * E)
                for h in range(NT // NG):
                    c4 = lambda a: a.rearrange("p (t e) f -> p t e f", e=E)
                    wv = w_r[:, h * NG:(h + 1) * NG, :]
                    other = wv.rearrange("p (t a) f -> p t a f", a=1).to_broadcast([P, NG, E, E])
                    own = wv.rearrange("p t (e a) -> p t e a", a=1).to_broadcast([P, NG, E, E])
                    less = cst[:, C_LESS:C_LESS + E * E].rearrange("p (a e f) -> p a e f", a=1, f=E)\
                        .to_broadcast([P, NG, E, E])
                    then(pool.tensor_tensor(c4(cb), other, own, ALU.subtract))
                    then(pool.tensor_scalar(ca, cb, 0.0, None, ALU.is_gt))
                    then(pool.tensor_scalar(cb, cb, 0.0, None, ALU.is_equal))
                    then(pool.tensor_tensor(c4(cb), c4(cb), less, ALU.mult))
                    then(pool.tensor_tensor(ca, ca, cb, ALU.add))
                    sum8(rank[:, h * NG:(h + 1) * NG, :].rearrange("p t e -> p (t e)"), ca, NG * E)
                then(pool.tensor_scalar(rank[:, :, :], rank[:, :, :], 2.0, None, ALU.is_lt))
                then(pool.tensor_tensor(w_r[:, :, :], rank[:, :, :], w_r[:, :, :], ALU.mult))
                then(pool.tensor_copy(ca, w_r[:, :, :]))
                sum8(rsm[:, :], ca, NT)
                then(pool.tensor_scalar(rss[:, :], rss[:, :], EPS_GATE, None, ALU.mult))
                then(pool.tensor_tensor(rss[:, :], rss[:, :], rsm[:, :], ALU.add))
                then(pool.tensor_tensor(rsm[:, :], rss[:, :], cst[:, C_MONE:C_MONE + NT], ALU.pow))
                then(pool.tensor_tensor(w_r[:, :, :], w_r[:, :, :],
                                        rsm[:, :].rearrange("p (t a) -> p t a", a=1).to_broadcast([P, NT, E]),
                                        ALU.mult))
                then(pool.tensor_copy(cwhl[:, :, 0:E], w_r[:, :, :]))
                pool.tensor_tensor(cwhl[:, :, E:2 * E], w_r[:, :, :], cwhl[:, :, 0:E].bitcast(F32), ALU.subtract)\
                    .then_inc(s["cw"], 1)

            def split_w(k):
                e, raw = k // 2, wraw[:, k % 2, :]
                hi, lo = ((w1h, w1l), (w2h, w2l))[k % 2]
                pool.wait_ge(ld["w1"] if k % 2 == 0 else ld["w2"], 16 * (e + 1))
                pool.tensor_copy(hi[:, bass.ts(e, F)], raw).then_inc(s["wh"], 1)
                pool.wait_ge(s["wh"], k + 1)
                pool.tensor_tensor(lo[:, bass.ts(e, F)], raw, hi[:, bass.ts(e, F)].bitcast(F32), ALU.subtract)\
                    .then_inc(s["wl"], 1)
            for k in range(2 * E):
                split_w(k)
            router()

            pool.wait_ge(s["xo"], NB)
            pool.wait_ge(ld["gam"], 16)
            pool.wait_ge(ld["bet"], 16)

            def finish(b, par, stored_before):
                pool.wait_ge(s["fmv"], b + 1)
                plain(pool)
                pool.tensor_scalar(fve[:, :], fmv[:, :, 1], EPS_LN, None, ALU.add).then_inc(s["fve"], 1)
                pool.wait_ge(s["fve"], b + 1)
                if not (isinstance(b, int) and b == 0):
                    pool.wait_ge(s["fz"], b)
                pool.tensor_tensor(frs[:, :], fve[:, :], half, ALU.pow).then_inc(s["frs"], 1)
                row = lambda a: a.rearrange("p (i d) -> p i d", i=TT)
                over = lambda a: a.rearrange("p (i d) -> p i d", i=1).to_broadcast([P, TT, D])
                pool.wait_ge(s["fz"], b + 1)
                o = row(fo[:, par, :])
                if not (isinstance(b, int) and b < 2):
                    pool.wait_ge(s_out[par], stored_before)
                pool.tensor_tensor(o, row(fz[:, :]), over(gam[:, :]), ALU.mult).then_inc(s["fg"], 1)
                pool.wait_ge(s["fg"], b + 1)
                pool.tensor_tensor(o, o, over(bet[:, :]), ALU.add).then_inc(s["fb"], 1)
                pool.wait_ge(s["fb"], b + 1)
                pool.wait_ge(s_xb[par], stored_before + 16)
                pool.tensor_tensor(o, o, row(xin[:, par, :]), ALU.add).then_inc(s["fo"], 1)

            def body_b(it):
                for par in range(2):
                    b = it * 2 + par
                    first = isinstance(b, int) and b == 0
                    if not first:
                        finish(b - 1, (par + 1) % 2, (it - 1 + par) * 16)
                    for e in range(1, E):
                        pool.wait_ge(s["yw"], b * E + e + 1)
                        if not (first and e == 1):
                            pool.wait_ge(s["fadd"], b * (E - 1) + e - 1)
                        pool.tensor_tensor(facc[:, :], facc[:, :], yw[:, e % 2, :], ALU.add).then_inc(s["fadd"], 1)
            trips(pool, body_b, 2)
            finish(NB - 1, 1, (NB // 2 - 1) * 16)


_INS = ["L0_attn_x", "L0_attn_Wc_down", "L0_attn_Wq_up", "L0_attn_Wkv_up", "L0_attn_Wc_proj", "L0_ffn_Wg",
        "L0_ffn_bg", "L0_ffn_W1", "L0_ffn_b1", "L0_ffn_W2", "L0_ffn_b2", "L0_ffn_gamma", "L0_ffn_beta"]


def kernel(**inputs):
    import numpy as _np
    import concourse.bacc as _bacc
    from concourse import mybir as _mybir
    from concourse.bass_utils import run_bass_kernel_spmd as _run

    const = _np.zeros((P, C_END), _np.float32)
    row = _np.arange(P)
    const[:, C_ID:C_ID + P] = _np.eye(P)
    const[:, C_CAUSAL:C_CAUSAL + P] = _np.where(row[None, :] <= row[:, None], 0.0, -1e30)
    const[:, C_CAUSALT:C_CAUSALT + P] = const[:, C_CAUSAL:C_CAUSAL + P].T
    const[:, C_NEGQ] = _np.where((row % 32 >= 2 * DH) & (row % 32 < 3 * DH), -1.0, 0.0)
    const[:, C_NEGK] = _np.where((row % 32 >= DH) & (row % 32 < 2 * DH), -1.0, 0.0)
    const[:, C_ONEK] = _np.where((row % 32 >= R_MAX) & (row % 32 < R_MAX + 2), 1.0, 0.0)
    const[:, C_HALF:C_HALF + TT] = -0.5
    const[:, C_MONE:C_MONE + NT] = -1.0
    const[:, C_LESS:C_LESS + E * E] = _np.tril(_np.ones((E, E)), -1).reshape(1, E * E)
    selc = _np.zeros((2 * E, E, P), _np.float32)
    for e in range(E):
        selc[e, e, :] = 1.0
        selc[E + e, e, :] = 1.0
    selc = selc.reshape(2 * E, E * P)

    nc = _bacc.Bacc("TRN2", target_bir_lowering=False, num_devices=1)
    arrays, args = {}, []
    for name, a in [(n, inputs[n]) for n in _INS] + [("const", const), ("selc", selc)]:
        a = _np.ascontiguousarray(a)
        arrays[f"in_{name}_dram"] = a
        args.append(nc.dram_tensor(f"in_{name}_dram", a.shape, _mybir.dt.from_np(a.dtype), kind="ExternalInput").ap())
    out = nc.dram_tensor("out_0_dram", (NB, T, D), _mybir.dt.float32, kind="ExternalOutput").ap()
    resid = nc.dram_tensor("resid", (NB, T, D), _mybir.dt.float32, kind="Internal").ap()
    build(nc, *args, resid, out)
    r = _run(nc, [arrays], core_ids=[0])
    return r.results[0]["out_0_dram"]
```

```python
from contextlib import ExitStack

import concourse.bass as bass
from concourse import mybir

F32 = mybir.dt.float32
F32R = mybir.dt.float32r
BF16 = mybir.dt.bfloat16
ALU = mybir.AluOpType
ACT = mybir.ActivationFunctionType
AX_X = mybir.AxisListType.X

P = 128
D = 128
NB = 16
T = 512
TT = T // P
NT = NB * TT
H = 16
DH = D // H
LAT = 64
G = 4
NJ = H // G
NSTEP = NB * NJ
E = 8
F = 512
FC = F // P
NC = E * FC
SCALE = 1.0 / float(DH) ** 0.5
EPS_LN = 1e-5
EPS_GATE = 1e-8

C_ID = 0
C_CAUSAL = C_ID + P
C_CAUSALT = C_CAUSAL + P
C_LOWQ = C_CAUSALT + P
C_LOWK = C_LOWQ + 1
C_HALF = C_LOWK + 1
C_MONE = C_HALF + TT
C_LESS = C_MONE + TT
C_END = C_LESS + E * E

R_MAX = 3 * DH
MX_UNITS = ((0, 0, 4), (1, 0, 2), (1, 2, 2)) + tuple((i, g, 1) for i in (2, 3) for g in range(G))
EX_UNITS = tuple((i, g, 1) for i in (0, 1) for g in range(G)) + ((2, 0, 2), (2, 2, 2), (3, 0, 4))
NU = len(MX_UNITS)
assert len(EX_UNITS) == NU
RING = 3
EX_DONE = tuple(1 + max(w for w in range(NU) if EX_UNITS[w][0] == i) for i in range(TT))


def bank_freed(w):
    before = [v - NU for v in range(NU) if v % RING == w % RING] + [v for v in range(w) if v % RING == w % RING]
    return before[-1] + 1


ROUTER_OPS = (5, 6, 5, 5)
KEY_DMAS = 16 * G
ROW_DMAS = 16 * 2 * TT
RING_H = 8
LW2 = 3
C_TURN = 8
C_STATS = C_TURN + 1
C_NORM = C_STATS + 3


def build(nc, x, wcd, wqu, wkvu, wcp, wg, bg, w1, b1, w2, b2, gamma, beta, const, selc, resid, out):
    with ExitStack() as ctx:
        def sb(name, shape, dt=F32, scope=ctx):
            return scope.enter_context(nc.sbuf_tensor(name, shape, dt))

        def sem(name):
            return ctx.enter_context(nc.semaphore(name))

        cst = sb("cst", [P, C_END])
        causal_t = sb("causal_t", [P, P], BF16)
        ident_b = sb("ident_b", [P, P], BF16)
        xin = sb("xin", [P, 2, T])
        xT = sb("xT", [P, NT * P])
        w1h = sb("w1h", [P, NC * P], F32R)
        w1l = sb("w1l", [P, NC * P], F32R)
        w2h = sb("w2h", [P, NC * P], F32R)
        w2l = sb("w2l", [P, NC * P], F32R)
        gam = sb("gam", [P, D])
        bet = sb("bet", [P, D])
        b1r = sb("b1r", [NC, P])
        b1T = sb("b1T", [P, NC])
        b2r = sb("b2r", [2 * E, D])
        b2h = sb("b2h", [2 * E, D], F32R)
        b2l = sb("b2l", [2 * E, D], F32R)
        cwhl = sb("cwhl", [P, NT, 2 * E], F32R)
        ident = cst[:, C_ID:C_ID + P]

        scope_a = ExitStack()
        A = lambda name, shape, dt=F32: sb(name, shape, dt, scope_a)
        wcp_s = A("wcp_s", [P, D])
        later = A("later", [P, T])
        masked = A("masked", [P, RING, T], BF16)
        wghl = A("wghl", [P, 2 * E], F32R)
        bgr = A("bgr", [P, E])
        wsth = A("wsth", [P, NJ + 1, P], F32R)
        wstl = A("wstl", [P, NJ + 1, P], F32R)
        stats = A("stats", [P, 2, TT, 6])
        mv = A("mv", [P, 2, TT, 2])
        veps = A("veps", [P, 2, TT])
        rstd = A("rstd", [P, 2, TT])
        xn = A("xn", [P, 2, T])
        xh = A("xh", [P, 2, T], F32R)
        xl = A("xl", [P, 2, T], F32R)
        lgs = A("lgs", [P, TT, 2, E])
        lg = A("lg", [P, TT, E])
        w_r = A("w_r", [P, 2, TT, E])
        rmx = A("rmx", [P, TT])
        rsm = A("rsm", [P, TT])
        rss = A("rss", [P, TT])
        rank = A("rank", [P, TT * E])
        cmp = A("cmp", [P, 2, TT * E * E])
        kpad = A("kpad", [P, 2, G, T], F32R)
        kh = A("kh", [P, T], F32R)
        kf = A("kf", [P, T], F32R)
        kvs = A("kvs", [P, T])
        vv = A("vv", [P, 2, TT, 32])
        qs = A("qs", [P, 4, T], F32R)
        qh = A("qh", [P, T], F32R)
        qr = A("qr", [P, T])
        pvs = A("pvs", [P, T])
        rden = A("rden", [P, TT * G])
        y = A("y", [P, 2, TT, D])
        yT = A("yT", [P, T])
        nm = A("nm", [P, G * TT])
        nmhl = A("nmhl", [P, 2, 2 * G * TT])
        nmh_r = A("nmh_r", [P, G * TT], F32R)
        ms = A("ms", [2 * G * TT, 2, P], F32R)
        wraw = A("wraw", [P, 2, F])
        scope_s = ExitStack()
        S = lambda name, shape, dt=F32: sb(name, shape, dt, scope_s)
        wcd_s = S("wcd_s", [P, LAT])
        wcdT = S("wcdT", [LAT, P])
        wup = S("wup", [LAT, D + 2 * DH])
        wg_s = S("wg_s", [P, E])
        wfold = S("wfold", [P, D + 2 * DH])
        wst = S("wst", [P, NJ + 1, P])
        ones = S("ones", [2, T], F32R)
        scope_s.close()
        pp = A("pp", [P, G * sum(T - i * P for i in range(TT))])

        def pp_tile(i):
            at, cols = G * sum(T - j * P for j in range(i)), T - i * P
            return pp[:, at:at + G * cols].rearrange("p (g c) -> p g c", g=G)
        scope_a.close()

        scope_b = ExitStack()
        B = lambda name, shape, dt=F32: sb(name, shape, dt, scope_b)
        zh = B("zh", [P, 2, T], F32R)
        zl = B("zl", [P, 2, T], F32R)
        selcw = B("selcw", [P, E * P])
        selr = B("selr", [P, E * P], F32R)
        cws = B("cws", [P, 2, T], F32R)
        cwb = B("cwb", [P, 2, T])
        hf = B("hf", [P, 4, T])
        hh = B("hh", [P, RING_H, T], F32R)
        hl = B("hl", [P, RING_H, T], F32R)
        yw = B("yw", [P, 2, T])
        facc = B("facc", [P, 2, T])
        fst = B("fst", [P, TT, 6])
        fmv = B("fmv", [P, TT, 2])
        fve = B("fve", [P, TT])
        frs = B("frs", [P, TT])
        fz = B("fz", [P, T])
        cwst = B("cwst", [P, TT * 2 * E])
        fo = B("fo", [P, 2, T])
        scope_b.close()

        ps = ctx.enter_context(nc.psum_tensor("ps", [P, 8, T], F32))
        PS_MX, PS_EX, PS_PV, PS_MISC = 0, RING, 2 * RING, 2 * RING + 1
        misc = ps[:, PS_MISC, :]

        dma_names = ("cst", "wcd", "wqu", "wkvu", "wcp", "wg", "bg", "w1", "b1", "w2", "b2", "gam", "bet", "sel", "ones")
        ld = {n: sem(f"s_ld_{n}") for n in dma_names}
        s_x = [sem(f"s_x{i}") for i in range(2)]
        s_xa = [sem(f"s_xa{i}") for i in range(2)]
        s_xr = [sem(f"s_xr{i}") for i in range(2)]
        s_xb = [sem(f"s_xb{i}") for i in range(2)]
        names = ("const_b", "later", "wcdT_ps", "wcdT", "fold_ps", "fold", "wst0", "wst", "wsth", "wstl", "wgh", "wgl", "kz",
                 "vz", "vone", "b1_ps", "b1T", "b2h", "b2l",
                 "stat", "mv", "veps", "rstd", "xn", "xT_ps", "xT", "lg_ps", "lgs", "lg1", "lg2", "rmx", "lt",
                 "rexp", "rp", "cw", "wh", "wl",
                 "xh", "xl", "kv_ps", "kh", "kvs", "kf", "v_ps", "v", "q_ps", "qh", "qr", "qs", "mx_ps", "mx", "nm1",
                 "nm", "mT_ps", "mT", "ex_ps", "ex", "pv", "pvs", "pvT_ps", "rden", "y", "yT_ps", "yT",
                 "c_ps", "xo",
                 "cz", "selr", "zh", "zl", "cwst", "ct_ps", "cws", "cb_ps", "cwb", "h_ps", "hf", "hh_a", "hh_d", "hl",
                 "y_ps", "yw", "fadd", "ft_ps", "fst", "fmv", "fve", "frs", "fz", "fg", "fb", "fo", "zero")
        s = {n: sem(f"s_{n}") for n in names}
        s_passed = sem("s_passed")
        s_kpad = [sem(f"s_kpad{i}") for i in range(2)]
        s_mrow = [sem(f"s_mrow{i}") for i in range(4)]
        s_out = [sem(f"s_out{i}") for i in range(2)]

        x_v = x.rearrange("b (i p) d -> b p i d", p=P)
        out_v = out.rearrange("b (i p) d -> b p i d", p=P)
        resid_v = resid.rearrange("b (i p) d -> b p i d", p=P)

        def seq_rows(view, b):
            return view[b, :, :, :] if isinstance(b, int) else \
                view[bass.ds(b, 1), :, :, :].rearrange("a p i d -> p (a i) d")

        def stage(it, u, lag, n_all, unroll, per=1):
            assert (u - lag) % per == 0
            n = it * (unroll // per) + (u - lag) // per
            if isinstance(it, int) and not 0 <= n < n_all:
                return None
            return n

        def trips(eng, body, head=1):
            for it in range(head):
                body(it)
            with eng.Fori(head, NB // 2 - 1) as it:
                body(it)
            body(NB // 2 - 1)

        def loops(eng, body, lags, n_steps, unroll, head=1):
            total = -(-(n_steps + max(lags)) // unroll)
            full = n_steps // unroll
            for it in range(head):
                body(it)
            with eng.Fori(head, full) as it:
                body(it)
            for it in range(full, total):
                body(it)

        block = ctx.enter_context(nc.Block())

        LAG = dict(x=0, st=1, xT=2, kv=3, kd=4, v=4, q=5, lg=5, mx=6, w=6, m=7, ex=8, r0=8, r1=9, r2=10, r3=11,
                    pvl=9, pvT=9, yT=13, c=14)
        SEQ = ("x", "st", "xT", "kv", "kd", "v", "lg", "w", "r0", "r1", "r2", "r3", "yT", "c")
        XSLOT = {LAG[w] % 4: w for w in ("kv", "v", "yT", "c")}
        X2SLOT = {LAG[w] % 4: w for w in ("xT", "lg")}

        def a_idx(it, u, what):
            per = 4 if what in SEQ else 1
            if (u - LAG[what]) % per:
                return None
            return stage(it, u, LAG[what], NB if per == 4 else NSTEP, 8, per)

        def a_par(u, what):
            per = 4 if what in SEQ else 1
            return (u - LAG[what]) // per

        def plain(eng):
            eng.sem_inc(s_passed, 1)

        def pair(b, it, u, what):
            return b // 2 if isinstance(b, int) else it + a_par(u, what) // 2

        def misc_freed(it, u, slot):
            order = ("m", "q", "pvT", "x", "x2")
            at = u * len(order) + order.index(slot)
            while True:
                at -= 1
                pu, ps_ = at // len(order), order[at % len(order)]
                if isinstance(it, int) and 8 * it + pu < 0:
                    return []
                what = {"x": XSLOT.get(pu % 4), "x2": X2SLOT.get(pu % 4)}.get(ps_, ps_)
                if what is None:
                    continue
                n = a_idx(it, pu, what)
                if n is None:
                    continue
                return {"q": [(s["qr"], n + 1)], "m": [(s["mT"], n + 1)], "pvT": [(s["y"], n + 1)],
                        "kv": [(s["kvs"], n + 1)], "v": [(s["v"], n + 1)],
                        "xT": [(s["xT"], n + 1)], "lg": [(s["lgs"], n + 1)],
                        "yT": [(s["yT"], n + 1)], "c": [(s["xo"], n + 1)]}[what]

        @block.sync
        def _(sp):
            sp.dma_start(cst[:, :], const).then_inc(ld["cst"], 16)
            sp.dma_start(wcd_s[:, :], wcd).then_inc(ld["wcd"], 16)
            sp.dma_start(wup[:, 0:D], wqu).then_inc(ld["wqu"], 16)
            sp.dma_start(wup[:, D:D + 2 * DH], wkvu).then_inc(ld["wkvu"], 16)
            sp.dma_start(xn[:, 0, :].rearrange("p (i d) -> p i d", i=TT), seq_rows(x_v, 0)).then_inc(s_x[0], 16)
            sp.dma_start(wcp_s[:, :], wcp).then_inc(ld["wcp"], 16)
            sp.dma_start(wg_s[:, :], wg).then_inc(ld["wg"], 16)
            sp.dma_start(bgr[:, :], bg.rearrange("(a e) -> a e", a=1).to_broadcast([P, E])).then_inc(ld["bg"], 16)
            sp.dma_start(b1r[:, :], b1.rearrange("e (c p) -> (e c) p", p=P)).then_inc(ld["b1"], 16)
            for r in range(2):
                sp.dma_start(b2r[r * E:(r + 1) * E, :], b2).then_inc(ld["b2"], 16)

            def load_w(k):
                e = k // 2
                if k >= 2:
                    sp.wait_ge(s["wl"], k - 1)
                if k % 2 == 0:
                    sp.dma_start(wraw[:, 0, :], w1[e, :, :]).then_inc(ld["w1"], 16)
                else:
                    sp.dma_start(wraw[:, 1, :].rearrange("p (c d) -> p c d", c=FC),
                                 w2[e, :, :].rearrange("(c p) d -> p c d", p=P)).then_inc(ld["w2"], 16)

            def rows(par):
                return xin[:, par, :].rearrange("p (i d) -> p i d", i=TT)

            def body(it):
                for u in range(8):
                    if isinstance(it, int) and 8 * it + u < 2 * E:
                        load_w(8 * it + u)
                    if isinstance(it, int) and 8 * it + u == 1:
                        sp.wait_ge(s["kz"], 2)
                        for par in range(2):
                            for g in range(G):
                                sp.dma_start(kpad[32 * g + R_MAX:32 * g + R_MAX + 2, par, g, :].bitcast(F32), ones[:, :].bitcast(F32))\
                                    .then_inc(ld["ones"], 16)
                    b = a_idx(it, u, "x")
                    if b is not None and not (isinstance(b, int) and b == 0):
                        par = a_par(u, "x") % 2
                        if not (isinstance(b, int) and b < 2):
                            sp.wait_ge(s["xT_ps"], b - 1)
                        sp.dma_start(xn[:, par, :].rearrange("p (i d) -> p i d", i=TT), seq_rows(x_v, b))\
                            .then_inc(s_x[par], 16)
                    n = a_idx(it, u, "m")
                    if n is not None:
                        r4 = a_par(u, "m") % 4
                        sp.wait_ge(s["mT"], n + 1)
                        for r in range(2):
                            for i in range(TT):
                                sp.dma_start(qs[R_MAX + r:P:32, r4, bass.ts(i, P)].bitcast(F32),
                                             ms[r * G * TT + i:(r + 1) * G * TT:TT, a_par(u, "m") % 2, :].bitcast(F32))\
                                    .then_inc(s_mrow[r4], 16)
                    b = a_idx(it, u, "kd")
                    if b is not None:
                        par = a_par(u, "kd") % 2
                        sp.wait_ge(s["kf"], b + 1)
                        if not (isinstance(b, int) and b < 2):
                            sp.wait_ge(s["ex_ps"], (4 * b - 4) * NU)
                        else:
                            sp.wait_ge(ld["ones"], 16 * 2 * G)
                        for g in range(G):
                            r = slice(32 * g, 32 * g + R_MAX)
                            sp.dma_start(kpad[r, par, g, :].bitcast(F32), kf[r, :].bitcast(F32))\
                                .then_inc(s_kpad[par], 16)
                    b = a_idx(it, u, "yT")
                    if b is not None:
                        par = a_par(u, "yT") % 2
                        if not (isinstance(b, int) and b < 2):
                            sp.wait_ge(s_xr[par], pair(b, it, u, "yT") * 16)
                        sp.dma_start(rows(par), seq_rows(x_v, b)).then_inc(s_xa[par], 16)
                    b = a_idx(it, u, "c")
                    if b is not None:
                        par = a_par(u, "c") % 2
                        sp.wait_ge(s["xo"], b + 1)
                        sp.dma_start(seq_rows(resid_v, b), rows(par)).then_inc(s_xr[par], 16)
            loops(sp, body, LAG.values(), NSTEP, 8, head=3)
            sp.dma_start(gam[:, :], gamma.rearrange("(a d) -> a d", a=1).to_broadcast([P, D])).then_inc(ld["gam"], 16)
            sp.dma_start(bet[:, :], beta.rearrange("(a d) -> a d", a=1).to_broadcast([P, D])).then_inc(ld["bet"], 16)
            for par in range(2):
                sp.wait_ge(s_xr[par], 16 * (NB // 2))
            sp.wait_ge(s["xo"], NB)
            sp.wait_ge(s["cz"], 1)
            sp.dma_start(selcw[0:2 * E, :], selc).then_inc(ld["sel"], 16)

            def body_b(it):
                for par in range(2):
                    b = it * 2 + par
                    if not (isinstance(b, int) and b < 2):
                        sp.wait_ge(s["fo"], b - 1)
                    sp.dma_start(rows(par), seq_rows(resid_v, b)).then_inc(s_xb[par], 16)
                    if not (isinstance(b, int) and b == 0):
                        store(b - 1, (par + 1) % 2)

            def store(b, par):
                sp.wait_ge(s["fo"], b + 1)
                sp.dma_start(seq_rows(out_v, b), fo[:, par, :].rearrange("p (i d) -> p i d", i=TT))\
                    .then_inc(s_out[par], 16)
            trips(sp, body_b)
            store(NB - 1, 1)
            for par in range(2):
                sp.wait_ge(s_out[par], 16 * (NB // 2))

        @block.tensor
        def _(pe):
            def mm3(o, ah, al, bh, bl, start=True, stop=True, skip=False):
                pe.matmul(o, ah, bh, start=start, stop=False, skip_group_check=skip)
                pe.matmul(o, ah, bl, start=False, stop=False, skip_group_check=skip)
                return pe.matmul(o, al, bh, start=False, stop=stop, skip_group_check=skip)

            pe.wait_ge(ld["cst"], 16)
            pe.wait_ge(ld["wcd"], 16)
            pe.transpose(ps[0:LAT, 0, 0:P], wcd_s[:, :], ident).then_inc(s["wcdT_ps"], 1)
            pe.wait_ge(s["wcdT"], 1)
            pe.wait_ge(ld["wqu"], 16)
            pe.wait_ge(ld["wkvu"], 16)
            pe.matmul(ps[:, 1, 0:D + 2 * DH], wcdT[:, :], wup[:, :], start=True, stop=True).then_inc(s["fold_ps"], 1)
            pe.wait_ge(ld["b1"], 16)
            pe.transpose(ps[:, 2, 0:NC], b1r[:, :], ident[0:NC, 0:NC]).then_inc(s["b1_ps"], 1)
            pe.wait_ge(s["wgl"], 1)
            pe.wait_ge(s["wstl"], 1)
            pe.wait_ge(s["const_b"], 2)
            pe.wait_ge(s["vone"], 1)
            pe.wait_ge(s["b1T"], 1)

            def misc_wait(it, u, slot):
                for sm, v in misc_freed(it, u, slot):
                    pe.wait_ge(sm, v)

            def body(it):
                for u in range(8):
                    n_mx, n_ex = a_idx(it, u, "mx"), a_idx(it, u, "ex")
                    masks = []

                    def max_scores(w):
                        i, g0, gn = MX_UNITS[w]
                        cols = (i + 1) * P
                        r4, kb = a_par(u, "mx") % 4, (a_par(u, "mx") // 4) % 2
                        if w == 0:
                            pe.wait_ge(s["qs"], n_mx + 1)
                            if a_par(u, "mx") % 4 == 0:
                                pe.wait_ge(s_kpad[kb], ((n_mx // 8 if isinstance(n_mx, int) else it + a_par(u, "mx") // 8)
                                                        + 1) * KEY_DMAS)
                        if not (isinstance(n_mx, int) and n_mx == 0 and w < RING):
                            pe.wait_ge(s["mx"], n_mx * NU + bank_freed(w))
                        heads = lambda a: a.rearrange("p (g c) -> p g c", g=gn)
                        o = heads(ps[:, PS_MX + w % RING, 0:gn * cols])
                        pe.matmul(o, qs[:, r4, bass.ts(i, P)], kpad[:, kb, g0:g0 + gn, 0:cols], start=True, stop=True,
                                  skip_group_check=True).then_inc(s["mx_ps"], 1)

                    def exp_scores(w):
                        i, g0, gn = EX_UNITS[w]
                        cols = T - i * P
                        r4, kb = a_par(u, "ex") % 4, (a_par(u, "ex") // 4) % 2
                        if w == 0:
                            pe.wait_ge(s_mrow[r4], (n_ex // 4 + 1) * ROW_DMAS if isinstance(n_ex, int) else
                                       (it * 2 + a_par(u, "ex") // 4 + 1) * ROW_DMAS)
                        if not (isinstance(n_ex, int) and n_ex == 0 and w < RING):
                            pe.wait_ge(s["ex"], n_ex * NU + bank_freed(w))
                        o = ps[:, PS_EX + w % RING, 0:gn * cols].rearrange("p (g c) -> p g c", g=gn)
                        for h in range(gn):
                            pe.matmul(o[:, h, :], kpad[:, kb, g0 + h, bass.ts(i, P)], qs[:, r4, i * P:T],
                                      start=(h == 0), stop=False, skip_group_check=True)
                        masks.append(o[:, :, 0:P])

                    def units(*ws):
                        masks.clear()
                        for w in ws:
                            if n_mx is not None:
                                max_scores(w)
                            if n_ex is not None:
                                exp_scores(w)
                        for o in masks:
                            mask = causal_t[:, :].rearrange("p (g c) -> p g c", g=1).to_broadcast([P, o.shape[1], P])
                            pe.matmul(o, ident_b[:, :], mask, start=False, stop=True, skip_group_check=True)\
                                .then_inc(s["ex_ps"], 1)

                    def pv(i, what="ex"):
                        n = a_idx(it, u, what)
                        if n is None:
                            return
                        vb = (a_par(u, what) // 4) % 2
                        if i == 0 and not (isinstance(n, int) and n == 0):
                            pe.wait_ge(s["pvs"], n)
                        pe.wait_ge(s["ex"], n * NU + EX_DONE[i])
                        for g in range(G):
                            mm = pe.matmul(ps[32 * g:32 * g + 32, PS_PV, i * P:T], vv[:, vb, i, :],
                                           pp_tile(i)[:, g, :], start=(i == 0), stop=(i == TT - 1))
                        mm.then_inc(s["pv"], 1)

                    def q_proj():
                        n = a_idx(it, u, "q")
                        if n is None:
                            return
                        misc_wait(it, u, "q")
                        j, kb = a_par(u, "q") % 4, (a_par(u, "q") // 4) % 2
                        mm3(misc, wsth[:, j, :], wstl[:, j, :], xh[:, kb, :], xl[:, kb, :]).then_inc(s["q_ps"], 1)

                    def max_rows():
                        n = a_idx(it, u, "m")
                        if n is None:
                            return
                        misc_wait(it, u, "m")
                        pe.wait_ge(s["nm"], n + 1)
                        pe.transpose(misc[0:2 * G * TT, 0:P], nmhl[:, a_par(u, "m") % 2, :], ident)\
                            .then_inc(s["mT_ps"], 1)

                    def pv_turn():
                        n = a_idx(it, u, "pvT")
                        if n is None:
                            return
                        misc_wait(it, u, "pvT")
                        pe.wait_ge(s["pvs"], n + 1)
                        for i in range(TT):
                            t = pe.transpose(misc[:, bass.ts(i, P)], pvs[:, bass.ts(i, P)], ident)
                        t.then_inc(s["pvT_ps"], 1)

                    def extra(slot):
                        what = (XSLOT if slot == "x" else X2SLOT).get(u % 4)
                        n = None if what is None else a_idx(it, u, what)
                        if n is None:
                            return
                        misc_wait(it, u, slot)
                        par = a_par(u, what) % 2
                        if what == "kv":
                            pe.wait_ge(s["xl"], n + 1)
                            mm3(misc, wsth[:, NJ, :], wstl[:, NJ, :], xh[:, par, :], xl[:, par, :])\
                                .then_inc(s["kv_ps"], 1)
                        elif what == "v":
                            pe.wait_ge(s["kvs"], n + 1)
                            for i in range(TT):
                                t = pe.transpose(misc[:, bass.ts(i, P)], kvs[:, bass.ts(i, P)], ident)
                            t.then_inc(s["v_ps"], 1)
                        elif what == "xT":
                            pe.wait_ge(s["xn"], n + 1)
                            for i in range(TT):
                                t = pe.transpose(misc[:, bass.ts(i, P)], xn[:, par, bass.ts(i, P)], ident)
                            t.then_inc(s["xT_ps"], 1)
                        elif what == "lg":
                            for i in range(TT):
                                o = misc[:, i * 2 * E:(i + 1) * 2 * E]
                                pe.matmul(o, xh[:, par, bass.ts(i, P)], wghl[:, :], start=True, stop=False)
                                t = pe.matmul(o[:, 0:E], xl[:, par, bass.ts(i, P)], wghl[:, 0:E],
                                              start=False, stop=True)
                            t.then_inc(s["lg_ps"], 1)
                        elif what == "yT":
                            for i in range(TT):
                                t = pe.transpose(misc[:, bass.ts(i, P)], y[:, par, i, :], ident)
                            t.then_inc(s["yT_ps"], 1)
                        else:
                            pe.wait_ge(s["yT"], n + 1)
                            for i in range(TT):
                                t = pe.matmul(misc[:, bass.ts(i, P)], yT[:, bass.ts(i, P)], wcp_s[:, :],
                                              start=True, stop=True)
                            t.then_inc(s["c_ps"], 1)

                    units(0)
                    pv(2, "pvl")
                    units(1)
                    max_rows()
                    units(2)
                    pv(3, "pvl")
                    units(3)
                    q_proj()
                    units(4, 5)
                    pv(0)
                    units(6)
                    pv_turn()
                    units(7, 8)
                    units(9)
                    extra("x")
                    units(10)
                    pv(1)
                    extra("x2")
            loops(pe, body, LAG.values(), NSTEP, 8, head=2)

            pe.wait_ge(s["wl"], 2 * E)
            pe.wait_ge(s["b2l"], 1)

            def turn_out(b, par):
                pe.wait_ge(s["fadd"], (b + 1) * (E - 1))
                if not (isinstance(b, int) and b == 0):
                    pe.wait_ge(s["fz"], b)
                for i in range(TT):
                    o = misc[:, bass.ts(i, P)]
                    pe.matmul(o, cws[0:2 * E, par, bass.ts(i, P)], b2h[:, :], start=True, stop=False)
                    pe.matmul(o, cws[0:2 * E, par, bass.ts(i, P)], b2l[:, :], start=False, stop=False)
                    t = pe.matmul(o, facc[:, par, bass.ts(i, P)], ident, start=False, stop=True)
                t.then_inc(s["ft_ps"], 1)

            def second(b, c):
                e, k = c // FC, c % FC
                if k == 0 and not (isinstance(b, int) and b == 0 and e < 2):
                    pe.wait_ge(s["yw"], b * E + e - 1)
                pe.wait_ge(s["hl"], b * NC + c + 1)
                mm3(ps[:, 4 + e % 2, :], w2h[:, bass.ts(c, P)], w2l[:, bass.ts(c, P)],
                    hh[:, c % RING_H, :], hl[:, c % RING_H, :], start=(k == 0), stop=(k == FC - 1))\
                    .then_inc(s["y_ps"], 1)

            def body_b(it):
                for par in range(2):
                    b = it * 2 + par
                    first = isinstance(b, int) and b == 0
                    for c in range(NC):
                        if c == 0:
                            pe.wait_ge(s["zl"], b + 1)
                        if not (first and c < 4):
                            pe.wait_ge(s["hf"], b * NC + c - 3)
                        mm3(ps[:, c % 4, :], w1h[:, bass.ts(c, P)], w1l[:, bass.ts(c, P)],
                            zh[:, par, :], zl[:, par, :]).then_inc(s["h_ps"], 1)
                        if c == 1:
                            pe.wait_ge(s["cwst"], b + 1)
                            if not first:
                                pe.wait_ge(s["cwb"], b * E)
                            for i in range(TT):
                                t = pe.transpose(ps[0:2 * E, 6, bass.ts(i, P)], cwst[:, bass.ts(i, 2 * E)], ident)
                            t.then_inc(s["ct_ps"], 1)
                        if c % FC == FC - 1:
                            e = c // FC
                            if e == 0:
                                pe.wait_ge(s["selr"], 1)
                                pe.wait_ge(s["cws"], b + 1)
                            else:
                                pe.wait_ge(s["cwb"], b * E + e)
                            pe.matmul(ps[:, 6, :], selr[:, bass.ts(e, P)], cws[:, par, :], start=True, stop=True)\
                                .then_inc(s["cb_ps"], 1)
                        if c == C_TURN and not first:
                            turn_out(b - 1, (par + 1) % 2)
                        if c >= LW2:
                            second(b, c - LW2)
                        elif not first:
                            second(b - 1, NC + c - LW2)
            trips(pe, body_b)
            for c in range(NC - LW2, NC):
                second(NB - 1, c)
            turn_out(NB - 1, 1)

        @block.scalar
        def _(act):
            def copy(o, i):
                return act.activation(o, i, ACT.Copy)

            act.wait_ge(ld["cst"], 16)
            copy(causal_t[:, :], cst[:, C_CAUSALT:C_CAUSALT + P]).then_inc(s["const_b"], 1)
            copy(ident_b[:, :], ident).then_inc(s["const_b"], 1)
            act.wait_ge(s["wcdT_ps"], 1)
            copy(wcdT[:, :], ps[0:LAT, 0, 0:P]).then_inc(s["wcdT"], 1)
            act.wait_ge(s["fold_ps"], 1)
            copy(wfold[:, :], ps[:, 1, 0:D + 2 * DH]).then_inc(s["fold"], 1)
            act.wait_ge(s["b1_ps"], 1)
            copy(b1T[:, :], ps[:, 2, 0:NC]).then_inc(s["b1T"], 1)
            act.wait_ge(ld["wg"], 16)
            copy(wghl[:, 0:E], wg_s[:, :]).then_inc(s["wgh"], 1)
            act.wait_ge(ld["b2"], 32)
            copy(b2h[:, :], b2r[:, :]).then_inc(s["b2h"], 1)
            act.wait_ge(s["wst"], 1)
            copy(wsth[:, :, :], wst[:, :, :]).then_inc(s["wsth"], 1)
            def body(it):
                for u in range(8):
                    n_ex = a_idx(it, u, "ex")
                    def exp_unit(w):
                        if n_ex is None:
                            return
                        i, g0, gn = EX_UNITS[w]
                        cols = T - i * P
                        act.wait_ge(s["ex_ps"], n_ex * NU + w + 1)
                        if g0 == 0 and not (isinstance(n_ex, int) and n_ex == 0):
                            act.wait_ge(s["pv"], (n_ex - 1) * TT + i + 1)
                        act.activation(pp_tile(i)[:, g0:g0 + gn, :],
                                       ps[:, PS_EX + w % RING, 0:gn * cols].rearrange("p (g c) -> p g c", g=gn),
                                       ACT.Exp, scale=SCALE).then_inc(s["ex"], 1)

                    exp_unit(0)
                    exp_unit(1)
                    n = a_idx(it, u, "m")
                    if n is not None:
                        act.wait_ge(s["mT_ps"], n + 1)
                        if not (isinstance(n, int) and n < 2):
                            r4 = (a_par(u, "m") - 2) % 4
                            act.wait_ge(s_mrow[r4], ((n - 2) // 4 + 1) * ROW_DMAS if isinstance(n, int) else
                                        (it * 2 + (a_par(u, "m") - 2) // 4 + 1) * ROW_DMAS)
                        copy(ms[:, a_par(u, "m") % 2, :], misc[0:2 * G * TT, 0:P]).then_inc(s["mT"], 1)
                    exp_unit(2)
                    n = a_idx(it, u, "pvT")
                    if n is not None:
                        act.wait_ge(s["pv"], (n + 1) * TT)
                        if not (isinstance(n, int) and n == 0):
                            act.wait_ge(s["pvT_ps"], n)
                        copy(pvs[:, :], ps[:, PS_PV, :]).then_inc(s["pvs"], 1)
                    exp_unit(3)
                    n = a_idx(it, u, "q")
                    if n is not None:
                        act.wait_ge(s["q_ps"], n + 1)
                        if not (isinstance(n, int) and n == 0):
                            act.wait_ge(s["qs"], n)
                        act.activation(qh[:, :], misc, ACT.Identity, scale=cst[:, C_LOWQ:C_LOWQ + 1])\
                            .then_inc(s["qh"], 1)
                        copy(qr[:, :], misc).then_inc(s["qr"], 1)
                    for w in range(4, 10):
                        exp_unit(w)
                    what = XSLOT[u % 4]
                    n = a_idx(it, u, what)
                    if n is not None:
                        par = a_par(u, what) % 2
                        if what == "kv":
                            act.wait_ge(s["kv_ps"], n + 1)
                            if not (isinstance(n, int) and n == 0):
                                act.wait_ge(s["kf"], n)
                                act.wait_ge(s["v_ps"], n)
                            act.activation(kh[:, :], misc, ACT.Identity, scale=cst[:, C_LOWK:C_LOWK + 1])\
                                .then_inc(s["kh"], 1)
                            copy(kvs[:, :], misc).then_inc(s["kvs"], 1)
                        elif what == "v":
                            act.wait_ge(s["v_ps"], n + 1)
                            if not (isinstance(n, int) and n < 2):
                                act.wait_ge(s["pv"], (4 * n - 4) * TT)
                            copy(vv[:, par, :, 0:DH], misc.rearrange("p (i c) -> p i c", i=TT)
                                 [:, :, R_MAX:R_MAX + DH]).then_inc(s["v"], 1)
                        elif what == "yT":
                            act.wait_ge(s["yT_ps"], n + 1)
                            if not (isinstance(n, int) and n == 0):
                                act.wait_ge(s["c_ps"], n)
                            copy(yT[:, :], misc).then_inc(s["yT"], 1)
                    for w in range(10, NU):
                        exp_unit(w)
                    b = a_idx(it, u, "xT")
                    if b is not None:
                        act.wait_ge(s["xT_ps"], b + 1)
                        if not (isinstance(b, int) and b < 2):
                            act.wait_ge(s["q_ps"], 4 * b - 4)
                            act.wait_ge(s["lg_ps"], b - 1)
                        copy(xh[:, a_par(u, "xT") % 2, :], misc).then_inc(s["xh"], 1)
                        copy(xT[:, bass.ts(b, T)], misc).then_inc(s["xT"], 1)
                    b = a_idx(it, u, "lg")
                    if b is not None:
                        act.wait_ge(s["lg_ps"], b + 1)
                        if not (isinstance(b, int) and b == 0):
                            act.wait_ge(s["lg2"], b)
                        copy(lgs[:, :, :, :].rearrange("p i r e -> p (i r e)"), misc[:, 0:TT * 2 * E])\
                            .then_inc(s["lgs"], 1)
                    b = a_idx(it, u, "w")
                    if b is not None:
                        act.wait_ge(s["lt"], b + 1)
                        w = w_r[:, a_par(u, "w") % 2, :, :]
                        act.activation(w, w, ACT.Exp).then_inc(s["rexp"], 1)
            loops(act, body, LAG.values(), NSTEP, 8, head=2)

            act.wait_ge(s["xo"], NB)
            def split_x(b, par, first):
                if not first:
                    act.wait_ge(s["h_ps"], (b - 1) * NC)
                copy(zh[:, par, :], xT[:, bass.ts(b, T)]).then_inc(s["zh"], 1)
            split_x(0, 0, True)

            def body_b(it):
                for par in range(2):
                    b = it * 2 + par
                    first = isinstance(b, int) and b == 0
                    if first:
                        act.wait_ge(s["cw"], NB)
                    else:
                        act.wait_ge(s["ct_ps"], b)
                    copy(cwst[:, :], cwhl[:, bass.ts(b, TT), :].bitcast(F32).rearrange("p i r -> p (i r)"))\
                        .then_inc(s["cwst"], 1)
                    for c in range(NC):
                        act.wait_ge(s["h_ps"], b * NC + c + 1)
                        if not (first and c < 4):
                            act.wait_ge(s["hl"], b * NC + c - 3)
                        act.activation(hf[:, c % 4, :], ps[:, c % 4, :], ACT.Gelu, bias=b1T[:, c:c + 1])\
                            .then_inc(s["hf"], 1)
                        if c % 2:
                            act.wait_ge(s["hf"], b * NC + c + 1)
                            if not (first and c < RING_H):
                                act.wait_ge(s["y_ps"], b * NC + c - RING_H + 1)
                            copy(hh[:, c % RING_H, :], hf[:, c % 4, :]).then_inc(s["hh_a"], 1)
                        if c == 1 and first:
                            act.wait_ge(ld["sel"], 16)
                            copy(selr[:, :], selcw[:, :]).then_inc(s["selr"], 1)
                        if c == 2:
                            act.wait_ge(s["ct_ps"], b + 1)
                            if not (isinstance(b, int) and b < 2):
                                act.wait_ge(s["ft_ps"], b - 1)
                            else:
                                act.wait_ge(s["cz"], 2)
                            copy(cws[0:2 * E, par, :], ps[0:2 * E, 6, :]).then_inc(s["cws"], 1)
                        if c % FC == FC - 1:
                            e = c // FC
                            act.wait_ge(s["cb_ps"], b * E + e + 1)
                            if not (first and e < 2):
                                act.wait_ge(s["yw"], b * E + e - 1)
                            copy(cwb[:, e % 2, :], ps[:, 6, :]).then_inc(s["cwb"], 1)
                        if c == NC // 2 and not (isinstance(b, int) and b == NB - 1):
                            split_x(b + 1, (par + 1) % 2, first)
            trips(act, body_b)

        @block.vector
        def _(dve):
            dve.memset(wst[:, :, :], 0.0).then_inc(s["wst0"], 1)
            dve.wait_ge(ld["cst"], 16)
            dve.memset(later[:, 0:T - P], 0.0)
            dve.tensor_copy(later[:, T - P:T], cst[:, C_CAUSAL:C_CAUSAL + P]).then_inc(s["later"], 1)
            dve.wait_ge(s["later"], 1)
            dve.wait_ge(s["fold"], 1)
            dve.wait_ge(s["wst0"], 1)
            for r in range(3):
                dve.tensor_copy(wst[:, 0:NJ, :].rearrange("p j (g c) -> p (j g) c", g=G)[:, :, r * DH:(r + 1) * DH],
                                wfold[:, 0:D].rearrange("p (h c) -> p h c", h=H))
                for g in range(G):
                    dve.tensor_copy(wst[:, NJ, 32 * g + r * DH:32 * g + (r + 1) * DH], wfold[:, D:D + DH])
            for g in range(G):
                t = dve.tensor_copy(wst[:, NJ, 32 * g + R_MAX:32 * g + R_MAX + DH], wfold[:, D + DH:D + 2 * DH])
            t.then_inc(s["wst"], 1)
            dve.wait_ge(s["wgh"], 1)
            dve.tensor_tensor(wghl[:, E:2 * E], wg_s[:, :], wghl[:, 0:E].bitcast(F32), ALU.subtract).then_inc(s["wgl"], 1)
            dve.wait_ge(ld["bg"], 16)
            dve.wait_ge(s["b2h"], 1)
            dve.tensor_tensor(b2l[:, :], b2r[:, :], b2h[:, :].bitcast(F32), ALU.subtract).then_inc(s["b2l"], 1)
            dve.wait_ge(s["wsth"], 1)
            dve.wait_ge(s["wst"], 1)
            dve.tensor_tensor(wstl[:, :, :], wst[:, :, :], wsth[:, :, :].bitcast(F32), ALU.subtract)\
                .then_inc(s["wstl"], 1)

            def body(it):
                for u in range(8):
                    n_mx = a_idx(it, u, "mx")
                    def reduce(w):
                        if n_mx is None:
                            return
                        i, g0, gn = MX_UNITS[w]
                        cols = (i + 1) * P
                        dve.wait_ge(s["mx_ps"], n_mx * NU + w + 1)
                        if w == 0 and not (isinstance(n_mx, int) and n_mx == 0):
                            dve.wait_ge(s["nm"], n_mx)
                        if w >= RING:
                            dve.wait_ge(s["mx"], n_mx * NU + w - RING + 1)
                        plain(dve)
                        for h in range(gn):
                            at = slice(h * cols, (h + 1) * cols)
                            r = dve.tensor_tensor_reduce(
                                out=masked[:, w % RING, at], in0=later[:, T - cols:T],
                                in1=ps[:, PS_MX + w % RING, at], scale=-1.0, scalar=3e38, op0=ALU.add, op1=ALU.min,
                                accum_out=nm[:, (g0 + h) * TT + i:(g0 + h) * TT + i + 1])
                        r.then_inc(s["mx"], 1)

                    for w in range(4):
                        reduce(w)
                    b = a_idx(it, u, "xT")
                    if b is not None:
                        par = a_par(u, "xT") % 2
                        dve.wait_ge(s["rstd"], b + 1)
                        dve.wait_ge(s["mv"], b + 1)
                        for i in range(TT):
                            xb = xn[:, par, bass.ts(i, D)]
                            t = dve.tensor_scalar(xb, xb, mv[:, par, i, 0:1], rstd[:, par, i:i + 1],
                                                  ALU.subtract, ALU.mult)
                        t.then_inc(s["xn"], 1)
                    for w in range(4, 7):
                        reduce(w)
                    n = a_idx(it, u, "pvT")
                    if n is not None:
                        par = a_par(u, "pvT")
                        dve.wait_ge(s["pvT_ps"], n + 1)
                        sums = misc.rearrange("p (n c) -> p n c", c=32)
                        dve.reciprocal(rden[:, :].rearrange("p (n a) -> p n a", a=1), sums[:, :, DH:DH + 1])\
                            .then_inc(s["rden"], 1)
                        dve.wait_ge(s["rden"], n + 1)
                        if par % 4 == 0 and not (isinstance(n, int) and n < 8):
                            dve.wait_ge(s["yT_ps"], (n if isinstance(n, int) else 0) // 4 - 1 if isinstance(n, int)
                                        else it * 2 + par // 4 - 1)
                        j = par % 4
                        dve.tensor_tensor(
                            y[:, (par // 4) % 2, :, j * G * DH:(j + 1) * G * DH].rearrange("p i (g c) -> p i g c", g=G),
                            misc.rearrange("p (i g c) -> p i g c", i=TT, g=G)[:, :, :, 0:DH],
                            rden[:, :].rearrange("p (i g a) -> p i g a", i=TT, a=1).to_broadcast([P, TT, G, DH]),
                            ALU.mult).then_inc(s["y"], 1)
                    reduce(7)
                    reduce(8)
                    reduce(9)
                    what = XSLOT[u % 4]
                    n = a_idx(it, u, what)
                    if n is not None and what == "c":
                        dve.wait_ge(s["c_ps"], n + 1)
                        par = a_par(u, what) % 2
                        dve.wait_ge(s_xa[par], (pair(n, it, u, what) + 1) * 16)
                        xb = xin[:, par, :]
                        dve.tensor_tensor(xb, xb, misc, ALU.add).then_inc(s["xo"], 1)
                    for w in range(10, NU):
                        reduce(w)
                    b = a_idx(it, u, "st")
                    if b is not None:
                        par = a_par(u, "st") % 2
                        dve.wait_ge(s_x[par], (pair(b, it, u, "st") + 1) * 16)
                        if not (isinstance(b, int) and b == 0):
                            dve.wait_ge(s["xn"], b)
                        for i in range(TT):
                            t = dve.bn_stats(stats[:, par, i, :], xn[:, par, bass.ts(i, D)])
                        t.then_inc(s["stat"], 1)
                        dve.wait_ge(s["stat"], b + 1)
                        plain(dve)
                        for i in range(TT):
                            t = dve.bn_aggr(mv[:, par, i, :], stats[:, par, i, :])
                        t.then_inc(s["mv"], 1)
                    if n_mx is not None:
                        par = a_par(u, "mx") % 2
                        dve.wait_ge(s["mx"], (n_mx + 1) * NU)
                        dve.tensor_copy(nmh_r[:, :], nm[:, :]).then_inc(s["nm1"], 1)
                        dve.wait_ge(s["nm1"], n_mx + 1)
                        if not (isinstance(n_mx, int) and n_mx < 2):
                            dve.wait_ge(s["mT_ps"], n_mx - 1)
                        dve.tensor_copy(nmhl[:, par, 0:G * TT], nmh_r[:, :].bitcast(F32))
                        dve.tensor_tensor(nmhl[:, par, G * TT:], nm[:, :], nmh_r[:, :].bitcast(F32), ALU.subtract)\
                            .then_inc(s["nm"], 1)
                    b = a_idx(it, u, "lg")
                    if b is not None:
                        dve.wait_ge(s["lgs"], b + 1)
                        if not (isinstance(b, int) and b == 0):
                            dve.wait_ge(s["lt"], b)
                        dve.tensor_tensor(lg[:, :, :], lgs[:, :, 1, :],
                                          bgr[:, :].rearrange("p (i e) -> p i e", i=1).to_broadcast([P, TT, E]),
                                          ALU.add).then_inc(s["lg1"], 1)
                        dve.wait_ge(s["lg1"], b + 1)
                        dve.tensor_tensor(lg[:, :, :], lg[:, :, :], lgs[:, :, 0, :], ALU.add).then_inc(s["lg2"], 1)
                        dve.wait_ge(s["lg2"], b + 1)
                        dve.tensor_reduce(rmx[:, :], lg[:, :, :], AX_X, ALU.max).then_inc(s["rmx"], 1)
                        dve.wait_ge(s["rmx"], b + 1)
                        if not (isinstance(b, int) and b < 2):
                            dve.wait_ge(s["cw"], b - 1)
                        dve.tensor_tensor(w_r[:, a_par(u, "lg") % 2, :, :], lg[:, :, :],
                                          rmx[:, :].rearrange("p (i a) -> p i a", a=1).to_broadcast([P, TT, E]),
                                          ALU.subtract).then_inc(s["lt"], 1)
            loops(dve, body, LAG.values(), NSTEP, 8, head=2)

            dve.wait_ge(s["c_ps"], NB)
            dve.wait_ge(s["xo"], NB)
            dve.wait_ge(s["cw"], NB)
            def split_x(b, par):
                dve.wait_ge(s["zh"], b + 1)
                dve.tensor_tensor(zl[:, par, :], xT[:, bass.ts(b, T)], zh[:, par, :].bitcast(F32), ALU.subtract)\
                    .then_inc(s["zl"], 1)
            split_x(0, 0)
            dve.memset(selcw[:, :], 0.0).then_inc(s["cz"], 1)
            dve.memset(cws[:, :, :].rearrange("p a t -> p (a t)").bitcast(F32), 0.0).then_inc(s["cz"], 1)

            def weigh(b, par, e):
                b_int = b if isinstance(b, int) else NB
                dve.wait_ge(s["y_ps"], b * NC + (e + 1) * FC)
                dve.wait_ge(s["cwb"], b * E + e + 1)
                if e == 0:
                    if b_int >= 2:
                        dve.wait_ge(s["ft_ps"], b - 1)
                    o = facc[:, par, :]
                else:
                    if not (b_int == 0 and e < 3):
                        dve.wait_ge(s["fadd"], b * (E - 1) + max(e - 2, 0))
                    o = yw[:, e % 2, :]
                dve.tensor_tensor(o, ps[:, 4 + e % 2, :], cwb[:, e % 2, :], ALU.mult).then_inc(s["yw"], 1)

            def out_stats(b):
                dve.wait_ge(s["ft_ps"], b + 1)
                if not (isinstance(b, int) and b == 0):
                    dve.wait_ge(s["fz"], b)
                for i in range(TT):
                    t = dve.bn_stats(fst[:, i, :], misc[:, bass.ts(i, D)])
                t.then_inc(s["fst"], 1)
                dve.wait_ge(s["fst"], b + 1)
                plain(dve)
                for i in range(TT):
                    t = dve.bn_aggr(fmv[:, i, :], fst[:, i, :])
                t.then_inc(s["fmv"], 1)

            def out_norm(b, i):
                if i == 0:
                    dve.wait_ge(s["frs"], b + 1)
                    dve.wait_ge(s["fmv"], b + 1)
                    if not (isinstance(b, int) and b == 0):
                        dve.wait_ge(s["fo"], b)
                t = dve.tensor_scalar(fz[:, bass.ts(i, D)], misc[:, bass.ts(i, D)], fmv[:, i, 0:1],
                                      frs[:, i:i + 1], ALU.subtract, ALU.mult)
                if i == TT - 1:
                    t.then_inc(s["fz"], 1)

            def body_b(it):
                for par in range(2):
                    b = it * 2 + par
                    first = isinstance(b, int) and b == 0
                    for c in range(NC):
                        dve.wait_ge(s["hf"], b * NC + c + 1)
                        if not (first and c < RING_H):
                            dve.wait_ge(s["y_ps"], b * NC + c - RING_H + 1)
                        h = hh[:, c % RING_H, :]
                        if c % 2 == 0:
                            dve.tensor_copy(h, hf[:, c % 4, :]).then_inc(s["hh_d"], 1)
                            dve.wait_ge(s["hh_d"], b * (NC // 2) + c // 2 + 1)
                        else:
                            dve.wait_ge(s["hh_a"], b * (NC // 2) + c // 2 + 1)
                        dve.tensor_tensor(hl[:, c % RING_H, :], hf[:, c % 4, :], h.bitcast(F32), ALU.subtract)\
                            .then_inc(s["hl"], 1)
                        if c % FC == LW2 - 1:
                            if c > FC:
                                weigh(b, par, c // FC - 1)
                            elif not first:
                                weigh(b - 1, (par + 1) % 2, E - 1)
                        if c == C_STATS and not first:
                            out_stats(b - 1)
                        if C_NORM <= c < C_NORM + TT and not first:
                            out_norm(b - 1, c - C_NORM)
                        if c == NC // 2 + 3 and not (isinstance(b, int) and b == NB - 1):
                            split_x(b + 1, (par + 1) % 2)
            trips(dve, body_b)
            weigh(NB - 1, 1, E - 1)
            out_stats(NB - 1)
            for i in range(TT):
                out_norm(NB - 1, i)

        @block.gpsimd
        def _(pool):
            half = cst[:, C_HALF:C_HALF + TT]
            pool.memset(kpad[:, :, :, :].rearrange("p a g t -> p (a g t)").bitcast(F32), 0.0).then_inc(s["kz"], 1)
            pool.memset(ones[:, :].bitcast(F32), 1.0).then_inc(s["kz"], 1)
            pool.memset(vv[:, :, :, :], 0.0).then_inc(s["vz"], 1)
            pool.wait_ge(s["vz"], 1)
            pool.memset(vv[:, :, :, DH:DH + 1], 1.0).then_inc(s["vone"], 1)
            pool.wait_ge(ld["cst"], 16)

            def deviations(b, par):
                pool.wait_ge(s["mv"], b + 1)
                if not (isinstance(b, int) and b < 2):
                    pool.wait_ge(s["xn"], b - 1)
                plain(pool)
                pool.tensor_scalar(veps[:, par, :], mv[:, par, :, 1], EPS_LN, None, ALU.add).then_inc(s["veps"], 1)
                pool.wait_ge(s["veps"], b + 1)
                pool.tensor_tensor(rstd[:, par, :], veps[:, par, :], half, ALU.pow).then_inc(s["rstd"], 1)

            def router(b, par, part):
                count = [sum(ROUTER_OPS[:part])]

                def then(ins):
                    count[0] += 1
                    ins.then_inc(s["rp"], 1)
                    pool.wait_ge(s["rp"], b * sum(ROUTER_OPS) + count[0])

                def sum8(o, full, a, n):
                    then(pool.tensor_tensor(a[:, 0:n, 0:4], full[:, :, 0:4], full[:, :, 4:8], ALU.add))
                    then(pool.tensor_tensor(a[:, 0:n, 0:2], a[:, 0:n, 0:2], a[:, 0:n, 2:4], ALU.add))
                    then(pool.tensor_tensor(o, a[:, 0:n, 0], a[:, 0:n, 1], ALU.add))

                w = w_r[:, par, :, :]
                ca = cmp[:, 0, :].rearrange("p (n f) -> p n f", f=E)
                cb = cmp[:, 1, :].rearrange("p (n f) -> p n f", f=E)
                c4 = lambda a: a.rearrange("p (t e) f -> p t e f", e=E)
                if part == 0:
                    pool.wait_ge(s["rexp"], b + 1)
                    sum8(rss[:, :], w, ca, TT)
                    other = w.rearrange("p t (a f) -> p t a f", a=1).to_broadcast([P, TT, E, E])
                    own = w.rearrange("p t (e a) -> p t e a", a=1).to_broadcast([P, TT, E, E])
                    then(pool.tensor_tensor(c4(cb), other, own, ALU.subtract))
                    plain(pool)
                    then(pool.tensor_scalar(ca, cb, 0.0, None, ALU.is_gt))
                if part == 1:
                    less = cst[:, C_LESS:C_LESS + E * E].rearrange("p (a e f) -> p a e f", a=1, f=E)\
                        .to_broadcast([P, TT, E, E])
                    then(pool.tensor_scalar(cb, cb, 0.0, None, ALU.is_equal))
                    then(pool.tensor_tensor(c4(cb), c4(cb), less, ALU.mult))
                    then(pool.tensor_tensor(ca, ca, cb, ALU.add))
                    sum8(rank[:, :], ca, ca, TT * E)
                if part == 2:
                    then(pool.tensor_scalar(rank[:, :], rank[:, :], 2.0, None, ALU.is_lt))
                    then(pool.tensor_tensor(w, rank[:, :].rearrange("p (t e) -> p t e", e=E), w, ALU.mult))
                    sum8(rsm[:, :], w, ca, TT)
                if part == 3:
                    then(pool.tensor_scalar(rss[:, :], rss[:, :], EPS_GATE, None, ALU.mult))
                    then(pool.tensor_tensor(rss[:, :], rss[:, :], rsm[:, :], ALU.add))
                    then(pool.tensor_tensor(rsm[:, :], rss[:, :], cst[:, C_MONE:C_MONE + TT], ALU.pow))
                    then(pool.tensor_tensor(w, w, rsm[:, :].rearrange("p (t a) -> p t a", a=1)
                                            .to_broadcast([P, TT, E]), ALU.mult))
                    hi = cwhl[:, bass.ts(b, TT), 0:E]
                    plain(pool)
                    then(pool.tensor_copy(hi, w))
                    pool.tensor_tensor(cwhl[:, bass.ts(b, TT), E:2 * E], w, hi.bitcast(F32), ALU.subtract)\
                        .then_inc(s["cw"], 1)
                assert count[0] == sum(ROUTER_OPS[:part + 1]), (part, count[0])

            def split_w(k):
                e, raw = k // 2, wraw[:, k % 2, :]
                hi, lo = ((w1h, w1l), (w2h, w2l))[k % 2]
                pool.wait_ge(ld["w1"] if k % 2 == 0 else ld["w2"], 16 * (e + 1))
                pool.tensor_copy(hi[:, bass.ts(e, F)], raw).then_inc(s["wh"], 1)
                pool.wait_ge(s["wh"], k + 1)
                pool.tensor_tensor(lo[:, bass.ts(e, F)], raw, hi[:, bass.ts(e, F)].bitcast(F32), ALU.subtract)\
                    .then_inc(s["wl"], 1)

            def body(it):
                for u in range(8):
                    n = a_idx(it, u, "q")
                    if n is not None:
                        pool.wait_ge(s["qh"], n + 1)
                        pool.wait_ge(s["qr"], n + 1)
                        if not (isinstance(n, int) and n < 4):
                            pool.wait_ge(s["ex_ps"], (n - 3) * NU)
                        plain(pool)
                        pool.tensor_tensor(qs[:, a_par(u, "q") % 4, :], qr[:, :], qh[:, :].bitcast(F32),
                                           ALU.subtract).then_inc(s["qs"], 1)
                    for part in range(4):
                        b = a_idx(it, u, f"r{part}")
                        if b is not None:
                            router(b, a_par(u, f"r{part}") % 2, part)
                    b = a_idx(it, u, "kv")
                    if b is not None:
                        pool.wait_ge(s["kh"], b + 1)
                        pool.wait_ge(s["kvs"], b + 1)
                        if not (isinstance(b, int) and b == 0):
                            before = a_par(u, "kv") - 1
                            pool.wait_ge(s_kpad[before % 2], ((b - 1) // 2 + 1) * KEY_DMAS if isinstance(b, int)
                                         else (it + before // 2 + 1) * KEY_DMAS)
                        plain(pool)
                        pool.tensor_tensor(kf[:, :], kvs[:, :], kh[:, :].bitcast(F32), ALU.subtract)\
                            .then_inc(s["kf"], 1)
                    b = a_idx(it, u, "st")
                    if b is not None:
                        deviations(b, a_par(u, "st") % 2)
                    b = a_idx(it, u, "xT")
                    if b is not None:
                        par = a_par(u, "xT") % 2
                        pool.wait_ge(s["xh"], b + 1)
                        pool.wait_ge(s["xT"], b + 1)
                        pool.tensor_tensor(xl[:, par, :], xT[:, bass.ts(b, T)], xh[:, par, :].bitcast(F32),
                                           ALU.subtract).then_inc(s["xl"], 1)
                    if isinstance(it, int) and 8 * it + u < 2 * E:
                        split_w(8 * it + u)
            loops(pool, body, (LAG["st"], LAG["r3"]), NSTEP, 8, head=2)

            pool.wait_ge(s["xo"], NB)
            pool.wait_ge(ld["gam"], 16)
            pool.wait_ge(ld["bet"], 16)

            def deviation_out(b):
                pool.wait_ge(s["fmv"], b + 1)
                plain(pool)
                pool.tensor_scalar(fve[:, :], fmv[:, :, 1], EPS_LN, None, ALU.add).then_inc(s["fve"], 1)
                pool.wait_ge(s["fve"], b + 1)
                if not (isinstance(b, int) and b == 0):
                    pool.wait_ge(s["fz"], b)
                pool.tensor_tensor(frs[:, :], fve[:, :], half, ALU.pow).then_inc(s["frs"], 1)

            def finish(b, par, stored_before):
                row = lambda a: a.rearrange("p (i d) -> p i d", i=TT)
                over = lambda a: a.rearrange("p (i d) -> p i d", i=1).to_broadcast([P, TT, D])
                pool.wait_ge(s["fz"], b + 1)
                o = row(fo[:, par, :])
                if not (isinstance(b, int) and b < 2):
                    pool.wait_ge(s_out[par], stored_before)
                pool.tensor_tensor(o, row(fz[:, :]), over(gam[:, :]), ALU.mult).then_inc(s["fg"], 1)
                pool.wait_ge(s["fg"], b + 1)
                pool.tensor_tensor(o, o, over(bet[:, :]), ALU.add).then_inc(s["fb"], 1)
                pool.wait_ge(s["fb"], b + 1)
                pool.wait_ge(s_xb[par], stored_before + 16)
                pool.tensor_tensor(o, o, row(xin[:, par, :]), ALU.add).then_inc(s["fo"], 1)

            def body_b(it):
                for par in range(2):
                    b = it * 2 + par
                    first = isinstance(b, int) and b == 0
                    if not first:
                        deviation_out(b - 1)
                    for e in range(1, E):
                        pool.wait_ge(s["yw"], b * E + e + 1)
                        if not (first and e == 1):
                            pool.wait_ge(s["fadd"], b * (E - 1) + e - 1)
                        acc = facc[:, par, :]
                        pool.tensor_tensor(acc, acc, yw[:, e % 2, :], ALU.add).then_inc(s["fadd"], 1)
                        if e == 2 and not first:
                            finish(b - 1, (par + 1) % 2, (it - 1 + par) * 16)
            trips(pool, body_b, 2)
            deviation_out(NB - 1)
            finish(NB - 1, 1, (NB // 2 - 1) * 16)


_INS = ["L0_attn_x", "L0_attn_Wc_down", "L0_attn_Wq_up", "L0_attn_Wkv_up", "L0_attn_Wc_proj", "L0_ffn_Wg",
        "L0_ffn_bg", "L0_ffn_W1", "L0_ffn_b1", "L0_ffn_W2", "L0_ffn_b2", "L0_ffn_gamma", "L0_ffn_beta"]


def kernel(**inputs):
    import numpy as _np
    import concourse.bacc as _bacc
    from concourse import mybir as _mybir
    from concourse.bass_utils import run_bass_kernel_spmd as _run

    const = _np.zeros((P, C_END), _np.float32)
    row = _np.arange(P)
    const[:, C_ID:C_ID + P] = _np.eye(P)
    const[:, C_CAUSAL:C_CAUSAL + P] = _np.where(row[None, :] <= row[:, None], 0.0, -1e30)
    const[:, C_CAUSALT:C_CAUSALT + P] = const[:, C_CAUSAL:C_CAUSAL + P].T
    const[:, C_LOWQ] = _np.where((row % 32 >= 2 * DH) & (row % 32 < 3 * DH), 1.0, 0.0)
    const[:, C_LOWK] = _np.where((row % 32 >= DH) & (row % 32 < 2 * DH), 1.0, 0.0)
    const[:, C_HALF:C_HALF + TT] = -0.5
    const[:, C_MONE:C_MONE + TT] = -1.0
    const[:, C_LESS:C_LESS + E * E] = _np.tril(_np.ones((E, E)), -1).reshape(1, E * E)
    selc = _np.zeros((2 * E, E, P), _np.float32)
    for e in range(E):
        selc[e, e, :] = 1.0
        selc[E + e, e, :] = 1.0
    selc = selc.reshape(2 * E, E * P)

    nc = _bacc.Bacc("TRN2", target_bir_lowering=False, num_devices=1)
    arrays, args = {}, []
    for name, a in [(n, inputs[n]) for n in _INS] + [("const", const), ("selc", selc)]:
        a = _np.ascontiguousarray(a)
        arrays[f"in_{name}_dram"] = a
        args.append(nc.dram_tensor(f"in_{name}_dram", a.shape, _mybir.dt.from_np(a.dtype), kind="ExternalInput").ap())
    out = nc.dram_tensor("out_0_dram", (NB, T, D), _mybir.dt.float32, kind="ExternalOutput").ap()
    resid = nc.dram_tensor("resid", (NB, T, D), _mybir.dt.float32, kind="Internal").ap()
    build(nc, *args, resid, out)
    r = _run(nc, [arrays], core_ids=[0])
    return r.results[0]["out_0_dram"]
```
